# Optimizing a Trainium2 kernel written in Bass

```python
import numpy as np
import jax
import jax.numpy as jnp

def _softmax(x, axis=-1):
    return jax.nn.softmax(x, axis=axis)

def _gelu(x):
    return jax.nn.gelu(x, approximate=True)

def _silu(x):
    return jax.nn.silu(x)

def _sigmoid(x):
    return jax.nn.sigmoid(x)

def _layernorm(x, axis=-1, eps=1e-05):
    m = jnp.mean(x, axis=axis, keepdims=True)
    v = jnp.var(x, axis=axis, keepdims=True)
    return (x - m) / jnp.sqrt(v + eps)

def _scatter_add(tgt, idx, src, axis=0):
    return tgt.at[idx].add(src)

def _segment_sum(src, seg, n):
    return jax.ops.segment_sum(src, seg, n)
kernel_name = 'mk_gnn_resnorm_d2_gnn_r8_b892a2'

def setup_inputs(seed: int=0):
    np.random.seed(seed)
    _w = jnp.asarray

    def _rec_inputs():
        import jax
        import jax.numpy as jnp
        _gk = jax.random.key(seed)
        x = -0.0005121 + 1.001 * jax.random.normal(jax.random.fold_in(_gk, 1), (12500, 32), jnp.float32)
        src = jax.random.randint(jax.random.fold_in(_gk, 2), (200000,), 0, 12500, jnp.int32)
        dst = jnp.minimum((12500 * jax.random.uniform(jax.random.fold_in(_gk, 3), (200000,)) ** 2.0).astype(jnp.int32), 99999)
        _o = jnp.argsort(dst, stable=True)
        src = src[_o]
        dst = dst[_o]
        edge_attr_3 = 0.000844983 + 0.999762 * jax.random.normal(jax.random.fold_in(_gk, 11), (200000, 3), jnp.float32)
        edge_attr_32 = 0.000216709 + 1.00012 * jax.random.normal(jax.random.fold_in(_gk, 12), (200000, 32), jnp.float32)
        edge_attr_4 = 0.000714719 + 1.00021 * jax.random.normal(jax.random.fold_in(_gk, 13), (200000, 4), jnp.float32)
        edge_weight = jax.random.uniform(jax.random.fold_in(_gk, 15), (200000,), jnp.float32, 0.0, 1)
        return (x, src, dst, edge_attr_3, edge_attr_32, edge_attr_4, edge_weight)
    x, src, dst, edge_attr_3, edge_attr_32, edge_attr_4, edge_weight = _rec_inputs()

    def _L0_gnn_setup():
        import jax, jax.numpy as jnp
        import numpy as np
        MUL = 8
        N_NODES = 12500
        N_EDGES = 100000
        EDGE_DIM = 32
        MLP_DIM = 64
        W_NUMEL = 4 * MUL * MUL
        ALPHA = 0.25
        C110 = 1.0 / np.sqrt(3.0)
        SI_SCALE = 1.0 / np.sqrt(MUL)
        key = jax.random.key(seed)
        ks = jax.random.split(key, 10)
        node_attr = jax.random.normal(ks[0], (N_NODES, 4 * MUL), dtype=jnp.float32)
        edge_index = jax.random.randint(ks[1], (2, N_EDGES), 0, N_NODES, dtype=jnp.int64)
        edge_sh = jax.random.normal(ks[2], (N_EDGES, 4), dtype=jnp.float32)
        edge_feat = jax.random.normal(ks[3], (N_EDGES, EDGE_DIM), dtype=jnp.float32)
        W1 = jax.random.normal(ks[4], (EDGE_DIM, MLP_DIM), dtype=jnp.float32) / np.sqrt(EDGE_DIM)
        b1 = jnp.zeros((MLP_DIM,), dtype=jnp.float32)
        W2 = jax.random.normal(ks[5], (MLP_DIM, W_NUMEL), dtype=jnp.float32) / np.sqrt(MLP_DIM)
        b2 = jnp.zeros((W_NUMEL,), dtype=jnp.float32)
        si_w0 = jax.random.normal(ks[6], (MUL, MUL), dtype=jnp.float32)
        si_w1 = jax.random.normal(ks[7], (MUL, MUL), dtype=jnp.float32)
        return {'node_attr': node_attr, 'edge_index': edge_index, 'edge_sh': edge_sh, 'edge_feat': edge_feat, 'W1': W1, 'b1': b1, 'W2': W2, 'b2': b2, 'si_w0': si_w0, 'si_w1': si_w1}
    _L0_gnn_all = _L0_gnn_setup()
    _L0_gnn_in = {k: v for k, v in _L0_gnn_all.items() if k in ('W1', 'b1', 'W2', 'b2', 'si_w0', 'si_w1')}
    del _L0_gnn_all

    def _L1_gnn_setup():
        import jax, jax.numpy as jnp
        import numpy as np
        from math import factorial, pi, sqrt
        MUL = 8
        RS = [(MUL, 0), (MUL, 1)]
        N_NODES = 2500
        N_EDGES = 80000
        FEAT_DIM = sum((m * (2 * l + 1) for m, l in RS))
        R_DIM = sum((mo * mi * (2 * min(lo, li) + 1) for mo, lo in RS for mi, li in RS))
        HIDDEN = 64

        def _cg(j1, j2, j3, m1, m2, m3):
            if m1 + m2 != m3:
                return 0.0
            f = factorial
            pre = sqrt((2 * j3 + 1) * f(j3 + j1 - j2) * f(j3 - j1 + j2) * f(j1 + j2 - j3) / f(j1 + j2 + j3 + 1))
            pre *= sqrt(f(j3 + m3) * f(j3 - m3) * f(j1 - m1) * f(j1 + m1) * f(j2 - m2) * f(j2 + m2))
            kmin = max(0, j2 - j3 - m1, j1 - j3 + m2)
            kmax = min(j1 + j2 - j3, j1 - m1, j2 + m2)
            s = 0.0
            for k in range(kmin, kmax + 1):
                s += (-1) ** k / (f(k) * f(j1 + j2 - j3 - k) * f(j1 - m1 - k) * f(j2 + m2 - k) * f(j3 - j2 + m1 + k) * f(j3 - j1 - m2 + k))
            return pre * s

        def _w3j_complex(l1, l2, l3):
            w = np.zeros((2 * l1 + 1, 2 * l2 + 1, 2 * l3 + 1))
            for m1 in range(-l1, l1 + 1):
                for m2 in range(-l2, l2 + 1):
                    m3 = -(m1 + m2)
                    if abs(m3) <= l3:
                        w[m1 + l1, m2 + l2, m3 + l3] = (-1) ** (l1 - l2 - m3) / sqrt(2 * l3 + 1) * _cg(l1, l2, l3, m1, m2, -m3)
            return w

        def _A(l):
            A = np.zeros((2 * l + 1, 2 * l + 1), dtype=complex)
            A[l, l] = 1.0
            for m in range(1, l + 1):
                A[l + m, l + m] = (-1) ** m / sqrt(2)
                A[l + m, l - m] = 1.0 / sqrt(2)
                A[l - m, l - m] = 1j / sqrt(2)
                A[l - m, l + m] = -1j * (-1) ** m / sqrt(2)
            return A

        def real_w3j(l1, l2, l3):
            wc = _w3j_complex(l1, l2, l3).astype(complex)
            wr = np.einsum('abc,ma,nb,oc->mno', wc, _A(l1).conj(), _A(l2).conj(), _A(l3).conj())
            i = int(np.argmax(np.abs(wr)))
            ph = wr.flat[i] / abs(wr.flat[i])
            wr = wr / ph
            assert np.abs(wr.imag).max() < 1e-10
            return np.real(wr).astype(np.float32)
        _W3J = {}
        for _mo, _lo in RS:
            for _mi, _li in RS:
                for _lf in range(abs(_lo - _li), _lo + _li + 1):
                    if (_lo, _lf, _li) not in _W3J:
                        _W3J[_lo, _lf, _li] = jnp.asarray(real_w3j(_lo, _lf, _li))
        _NORM = []
        for _mo, _lo in RS:
            _num = sum((mi * (2 * min(_lo, li) + 1) for mi, li in RS))
            _NORM.append(sqrt(4.0 * pi) * sqrt(2.0 * _lo + 1.0) / sqrt(_num))
        _F_OFFS = [0] + list(np.cumsum([mi * (2 * li + 1) for mi, li in RS]))

        def spherical_harmonics(rel_vec):
            r = rel_vec / jnp.linalg.norm(rel_vec, axis=-1, keepdims=True)
            x, y, z = (r[:, 0], r[:, 1], r[:, 2])
            y0 = jnp.full_like(x, 0.5 / sqrt(pi))[:, None]
            c1 = sqrt(3.0 / (4.0 * pi))
            y1 = c1 * jnp.stack([y, z, x], axis=-1)
            c2a = 0.5 * sqrt(15.0 / pi)
            c2b = 0.25 * sqrt(5.0 / pi)
            c2c = 0.25 * sqrt(15.0 / pi)
            y2 = jnp.stack([c2a * x * y, c2a * y * z, c2b * (3.0 * z * z - 1.0), c2a * x * z, c2c * (x * x - y * y)], axis=-1)
            return jnp.concatenate([y0, y1, y2], axis=-1)
        key = jax.random.key(seed)
        ks = jax.random.split(key, 6)
        features = jax.random.normal(ks[0], (N_NODES, FEAT_DIM), dtype=jnp.float32)
        abs_distances = jax.random.uniform(ks[1], (N_EDGES,), dtype=jnp.float32, minval=0.1, maxval=1.0)
        rel_vec = jax.random.normal(ks[2], (N_EDGES, 3), dtype=jnp.float32)
        edge_index = jax.random.randint(ks[3], (2, N_EDGES), 0, N_NODES, dtype=jnp.int32)
        w1 = jax.random.normal(ks[4], (1, HIDDEN), dtype=jnp.float32)
        b1 = jnp.zeros((HIDDEN,), jnp.float32)
        w2 = jax.random.normal(ks[5], (HIDDEN, R_DIM), dtype=jnp.float32) / sqrt(HIDDEN)
        b2 = jnp.zeros((R_DIM,), jnp.float32)
        return {'features': features, 'abs_distances': abs_distances, 'rel_vec': rel_vec, 'edge_index': edge_index, 'w1': w1, 'b1': b1, 'w2': w2, 'b2': b2}
    _L1_gnn_all = _L1_gnn_setup()
    _L1_gnn_in = {k: v for k, v in _L1_gnn_all.items() if k in ('w1', 'b1', 'w2', 'b2')}
    del _L1_gnn_all
    return {'x': x, 'src': src, 'dst': dst, 'edge_attr_3': edge_attr_3, 'edge_attr_32': edge_attr_32, 'edge_attr_4': edge_attr_4, 'edge_weight': edge_weight, 'L0_gnn_W1': _L0_gnn_in['W1'], 'L0_gnn_b1': _L0_gnn_in['b1'], 'L0_gnn_W2': _L0_gnn_in['W2'], 'L0_gnn_b2': _L0_gnn_in['b2'], 'L0_gnn_si_w0': _L0_gnn_in['si_w0'], 'L0_gnn_si_w1': _L0_gnn_in['si_w1'], 'L1_gnn_w1': _L1_gnn_in['w1'], 'L1_gnn_b1': _L1_gnn_in['b1'], 'L1_gnn_w2': _L1_gnn_in['w2'], 'L1_gnn_b2': _L1_gnn_in['b2']}

def reference(x, src, dst, edge_attr_3, edge_attr_32, edge_attr_4, edge_weight, L0_gnn_W1, L0_gnn_b1, L0_gnn_W2, L0_gnn_b2, L0_gnn_si_w0, L0_gnn_si_w1, L1_gnn_w1, L1_gnn_b1, L1_gnn_w2, L1_gnn_b2):
    import jax
    import jax.numpy as jnp

    def _L0_gnn_ref(node_attr, edge_index, edge_sh, edge_feat, W1, b1, W2, b2, si_w0, si_w1):
        import jax, jax.numpy as jnp
        import numpy as np
        MUL = 8
        N_NODES = 12500
        N_EDGES = 100000
        EDGE_DIM = 32
        MLP_DIM = 64
        W_NUMEL = 4 * MUL * MUL
        ALPHA = 0.25
        C110 = 1.0 / np.sqrt(3.0)
        SI_SCALE = 1.0 / np.sqrt(MUL)
        n = node_attr.shape[0]
        e = edge_sh.shape[0]
        h = jax.nn.relu(edge_feat @ W1 + b1)
        w = (h @ W2 + b2).reshape(e, 4, MUL, MUL)
        w_000, w_011, w_101, w_110 = (w[:, 0], w[:, 1], w[:, 2], w[:, 3])
        s = node_attr[:, :MUL]
        v = node_attr[:, MUL:].reshape(n, MUL, 3)
        src, dst = (edge_index[0], edge_index[1])
        s_e = s[src]
        v_e = v[src]
        sh0 = edge_sh[:, 0]
        sh1 = edge_sh[:, 1:4]
        m0 = ALPHA * (jnp.einsum('ei,eio->eo', s_e * sh0[:, None], w_000) + C110 * jnp.einsum('eim,em,eio->eo', v_e, sh1, w_110))
        m1 = ALPHA * (jnp.einsum('ei,em,eio->eom', s_e, sh1, w_011) + jnp.einsum('eim,eio->eom', v_e * sh0[:, None, None], w_101))
        out0 = jax.ops.segment_sum(m0, dst, num_segments=n)
        out1 = jax.ops.segment_sum(m1.reshape(e, MUL * 3), dst, num_segments=n).reshape(n, MUL, 3)
        out0 = out0 + SI_SCALE * (s @ si_w0)
        out1 = out1 + SI_SCALE * jnp.einsum('nim,io->nom', v, si_w1)
        return jnp.concatenate([out0, out1.reshape(n, MUL * 3)], axis=-1)

    def _L1_gnn_ref(features, abs_distances, rel_vec, edge_index, w1, b1, w2, b2):
        import jax, jax.numpy as jnp
        import numpy as np
        from math import factorial, pi, sqrt
        MUL = 8
        RS = [(MUL, 0), (MUL, 1)]
        N_NODES = 2500
        N_EDGES = 80000
        FEAT_DIM = sum((m * (2 * l + 1) for m, l in RS))
        R_DIM = sum((mo * mi * (2 * min(lo, li) + 1) for mo, lo in RS for mi, li in RS))
        HIDDEN = 64

        def _cg(j1, j2, j3, m1, m2, m3):
            if m1 + m2 != m3:
                return 0.0
            f = factorial
            pre = sqrt((2 * j3 + 1) * f(j3 + j1 - j2) * f(j3 - j1 + j2) * f(j1 + j2 - j3) / f(j1 + j2 + j3 + 1))
            pre *= sqrt(f(j3 + m3) * f(j3 - m3) * f(j1 - m1) * f(j1 + m1) * f(j2 - m2) * f(j2 + m2))
            kmin = max(0, j2 - j3 - m1, j1 - j3 + m2)
            kmax = min(j1 + j2 - j3, j1 - m1, j2 + m2)
            s = 0.0
            for k in range(kmin, kmax + 1):
                s += (-1) ** k / (f(k) * f(j1 + j2 - j3 - k) * f(j1 - m1 - k) * f(j2 + m2 - k) * f(j3 - j2 + m1 + k) * f(j3 - j1 - m2 + k))
            return pre * s

        def _w3j_complex(l1, l2, l3):
            w = np.zeros((2 * l1 + 1, 2 * l2 + 1, 2 * l3 + 1))
            for m1 in range(-l1, l1 + 1):
                for m2 in range(-l2, l2 + 1):
                    m3 = -(m1 + m2)
                    if abs(m3) <= l3:
                        w[m1 + l1, m2 + l2, m3 + l3] = (-1) ** (l1 - l2 - m3) / sqrt(2 * l3 + 1) * _cg(l1, l2, l3, m1, m2, -m3)
            return w

        def _A(l):
            A = np.zeros((2 * l + 1, 2 * l + 1), dtype=complex)
            A[l, l] = 1.0
            for m in range(1, l + 1):
                A[l + m, l + m] = (-1) ** m / sqrt(2)
                A[l + m, l - m] = 1.0 / sqrt(2)
                A[l - m, l - m] = 1j / sqrt(2)
                A[l - m, l + m] = -1j * (-1) ** m / sqrt(2)
            return A

        def real_w3j(l1, l2, l3):
            wc = _w3j_complex(l1, l2, l3).astype(complex)
            wr = np.einsum('abc,ma,nb,oc->mno', wc, _A(l1).conj(), _A(l2).conj(), _A(l3).conj())
            i = int(np.argmax(np.abs(wr)))
            ph = wr.flat[i] / abs(wr.flat[i])
            wr = wr / ph
            assert np.abs(wr.imag).max() < 1e-10
            return np.real(wr).astype(np.float32)
        _W3J = {}
        for _mo, _lo in RS:
            for _mi, _li in RS:
                for _lf in range(abs(_lo - _li), _lo + _li + 1):
                    if (_lo, _lf, _li) not in _W3J:
                        _W3J[_lo, _lf, _li] = jnp.asarray(real_w3j(_lo, _lf, _li))
        _NORM = []
        for _mo, _lo in RS:
            _num = sum((mi * (2 * min(_lo, li) + 1) for mi, li in RS))
            _NORM.append(sqrt(4.0 * pi) * sqrt(2.0 * _lo + 1.0) / sqrt(_num))
        _F_OFFS = [0] + list(np.cumsum([mi * (2 * li + 1) for mi, li in RS]))

        def spherical_harmonics(rel_vec):
            r = rel_vec / jnp.linalg.norm(rel_vec, axis=-1, keepdims=True)
            x, y, z = (r[:, 0], r[:, 1], r[:, 2])
            y0 = jnp.full_like(x, 0.5 / sqrt(pi))[:, None]
            c1 = sqrt(3.0 / (4.0 * pi))
            y1 = c1 * jnp.stack([y, z, x], axis=-1)
            c2a = 0.5 * sqrt(15.0 / pi)
            c2b = 0.25 * sqrt(5.0 / pi)
            c2c = 0.25 * sqrt(15.0 / pi)
            y2 = jnp.stack([c2a * x * y, c2a * y * z, c2b * (3.0 * z * z - 1.0), c2a * x * z, c2c * (x * x - y * y)], axis=-1)
            return jnp.concatenate([y0, y1, y2], axis=-1)
        src, dst = (edge_index[0], edge_index[1])
        R = jax.nn.relu(abs_distances[:, None] @ w1 + b1) @ w2 + b2
        Y = spherical_harmonics(rel_vec)
        Fj = features[src]
        E = Fj.shape[0]
        msg_blocks = []
        r_off = 0
        for i, (mo, lo) in enumerate(RS):
            acc = jnp.zeros((E, mo, 2 * lo + 1), dtype=features.dtype)
            for j, (mi, li) in enumerate(RS):
                n_lf = 2 * min(lo, li) + 1
                sz = mo * mi * n_lf
                Rb = R[:, r_off:r_off + sz].reshape(E, mo, mi, n_lf)
                r_off += sz
                Fb = Fj[:, _F_OFFS[j]:_F_OFFS[j + 1]].reshape(E, mi, 2 * li + 1)
                for k, lf in enumerate(range(abs(lo - li), lo + li + 1)):
                    C = _W3J[lo, lf, li]
                    Yf = Y[:, lf * lf:(lf + 1) * (lf + 1)]
                    acc = acc + _NORM[i] * jnp.einsum('euv,ef,evi,ofi->euo', Rb[..., k], Yf, Fb, C)
            msg_blocks.append(acc.reshape(E, -1))
        msg = jnp.concatenate(msg_blocks, axis=-1)
        out = jnp.zeros((features.shape[0], msg.shape[1]), dtype=features.dtype)
        out = out.at[dst].add(msg)
        return out
    edge_index = jnp.stack([src, dst])
    x = _layernorm(x + _L0_gnn_ref(x, edge_index, edge_attr_4, edge_attr_32, L0_gnn_W1, L0_gnn_b1, L0_gnn_W2, L0_gnn_b2, L0_gnn_si_w0, L0_gnn_si_w1), axis=-1)
    x = _layernorm(x + _L1_gnn_ref(x, edge_weight, edge_attr_3, edge_index, L1_gnn_w1, L1_gnn_b1, L1_gnn_w2, L1_gnn_b2), axis=-1)
    return x

_drawn_inputs = setup_inputs


def setup_inputs(seed=0):
    import zlib

    import numpy as np

    out = dict(_drawn_inputs(seed))
    spreads = {'L0_gnn_b1': (0.0, 0.1),
     'L0_gnn_b2': (0.0, 0.1),
     'L1_gnn_b1': (0.0, 0.1),
     'L1_gnn_b2': (0.0, 0.1)}
    factors = {}
    for name, (base, spread) in spreads.items():
        noise = np.random.default_rng([zlib.crc32(name.encode()), seed]).standard_normal(out[name].shape)
        drawn = base * np.exp(spread * noise) if base else spread * noise
        out[name] = jnp.asarray(drawn.astype(out[name].dtype))
    for name, factor in factors.items():
        out[name] = (out[name] * factor).astype(out[name].dtype)
    return out
```

```python
from contextlib import ExitStack
from math import pi, sqrt

import numpy as np

import concourse.bass as bass
from concourse import mybir

F32, BF16, I32 = mybir.dt.float32, mybir.dt.bfloat16, mybir.dt.int32
ALU = mybir.AluOpType
ACT = mybir.ActivationFunctionType
AX_X = mybir.AxisListType.X

P = 128
N_NODES, N_EDGES = 12500, 200000
MUL, FEAT = 8, 32
HID = 64
TILES = 8
CHUNK = TILES * P
RING = 4
CHUNKS = -(-N_EDGES // (CHUNK * RING)) * RING
ROUNDS = CHUNKS // RING
EDGES = CHUNKS * CHUNK
GROUP_TILES = 4
GROUPS = TILES // GROUP_TILES
N_GROUPS = CHUNKS * GROUPS
GROUP = GROUP_TILES * P
DST_ROWS = EDGES // (4 * GROUP)
BLOCKS = -(-N_NODES // P)
WINDOW = 2
PASSES_ALL = BLOCKS // WINDOW
SELF_CHUNKS = -(-BLOCKS // 4)
AHEAD = 1
MLP_USES = (ROUNDS + AHEAD, *[ROUNDS] * (RING - 1))
LN_EPS = 1e-5

W_COLS = (4 * MUL * MUL, 6 * MUL * MUL)
PROD_COLS = (6 * MUL * MUL, 10 * MUL * MUL)
SUM_COLS = (6 * MUL, 5 * MUL)
HALF_TILES = (4, 2)
HALVES = tuple(TILES // h for h in HALF_TILES)
HALVES_READY = tuple(CHUNKS * h + 2 for h in HALVES)
SCATTERS = (CHUNKS + 1) * GROUPS
ALPHA, C110, SI_SCALE = 0.25, 1.0 / sqrt(3.0), 1.0 / sqrt(MUL)
NORM0 = sqrt(4 * pi) / sqrt(2 * MUL)
NORM1 = sqrt(4 * pi) * sqrt(3.0) / sqrt(4 * MUL)
Y0, Y1 = 0.5 / sqrt(pi), sqrt(3.0 / (4 * pi))
K_00 = NORM0 * Y0
K_01 = NORM0 * Y1 / sqrt(3.0)
K_10 = NORM1 * Y1 / sqrt(3.0)
K_11_0 = NORM1 * Y0 / sqrt(3.0)
K_11_1 = NORM1 * Y1 / sqrt(6.0)
K_11_2 = NORM1 * sqrt(3.0 / (8 * pi))


class Steps:

    def __init__(self, eng, sem, base=0):
        self.eng, self.sem, self.base, self.n = eng, sem, base, 0

    def done(self, instruction):
        instruction.then_inc(self.sem, 1)
        self.n += 1
        return self.n

    def need(self, n):
        self.eng.wait_ge(self.sem, self.base + n)


def build(nc, x, x_nodes, x_self, src, dst, dst_rows, sh, feat, rel, dist, w1_0, b1_0, w2_0, si, w1_1, b1_1, w2_1,
          out):
    x1 = nc.dram_tensor("x1_rows", [BLOCKS * P, FEAT], F32).ap()
    y_dram = nc.dram_tensor("unit_vectors", [P, CHUNKS * TILES * 5], F32).ap()
    off_dram = nc.dram_tensor("window_offsets", [N_GROUPS], I32).ap()
    lo_dram = nc.dram_tensor("window_starts", [N_GROUPS], F32).ap()

    with ExitStack() as ctx:
        def sb(name, shape, dt=F32):
            return ctx.enter_context(nc.sbuf_tensor(name, shape, dt))

        def psum(name, shape, dt=F32):
            return ctx.enter_context(nc.psum_tensor(name, shape, dt))

        def sem(name):
            return ctx.enter_context(nc.semaphore(name))

        table = sb("table", [P, BLOCKS, FEAT])
        work = sb("work", [P, max(CHUNKS * TILES * 3, BLOCKS * FEAT, 8 * GROUP)])
        rel_sb = sb("rel_sb", [P, CHUNKS * TILES, 3])
        y_all = sb("y_all", [P, CHUNKS * TILES, 5])
        dst_i = sb("dst_i", [DST_ROWS, 4 * GROUP], I32)
        starts = sb("starts", [P, N_GROUPS])
        offs = sb("offs", [1, GROUPS + N_GROUPS], I32)
        xs = sb("xs", [P, SELF_CHUNKS, P])
        si_sb = sb("si_sb", [P, P])
        w1_sb = sb("w1_sb", [P, 4, HID])
        b1_sb = sb("b1_sb", [HID, 2])
        w1c_sb = sb("w1c_sb", [HID, 1])
        w2_sb = [sb(f"w2_sb{n}", [P, W_COLS[n]]) for n in range(2)]
        w2_tmp = sb("w2_tmp", [P, MUL, MUL])
        iota = sb("iota", [P, WINDOW * P])
        zeros = sb("zeros", [P, P], BF16)
        eps = sb("eps", [P, 1])
        lowest = sb("lowest", [DST_ROWS, 4])
        highest = sb("highest", [DST_ROWS, 4])
        span = sb("span", [DST_ROWS, 4])
        span_max = sb("span_max", [DST_ROWS, 2])
        fits = sb("fits", [DST_ROWS, 1])
        passes_f = sb("passes_f", [DST_ROWS, 1])
        passes_i = sb("passes_i", [DST_ROWS, 1], I32)
        off_f = sb("off_f", [DST_ROWS, 4])
        off_i = sb("off_i", [DST_ROWS, 4], I32)
        lo_f = sb("lo_f", [DST_ROWS, 4])
        node_a = sb("node_a", [P, BLOCKS])
        node_b = sb("node_b", [P, BLOCKS])
        node_c = sb("node_c", [P, BLOCKS])
        src_sb = [sb(f"src{z}", [P, TILES], I32) for z in range(RING)]
        dst_sb = [sb(f"dst{z}", [P, TILES], I32) for z in range(RING)]
        geo_sb = [sb(f"geo{z}", [P, TILES, 5]) for z in range(RING)]
        mlp_sb = [sb(f"mlp{z}", [P, CHUNK]) for z in range(RING)]
        rows = [sb(f"rows{z}", [P, TILES, FEAT]) for z in range(RING)]
        hidden = [sb(f"hidden{b}", [P, CHUNK]) for b in range(2)]
        ndst = [sb(f"ndst{b}", [P, TILES]) for b in range(2)]
        gap = [sb(f"gap{b}", [P, GROUP_TILES, WINDOW * P], BF16) for b in range(2)]
        onehot = [sb(f"onehot{b}", [P, TILES, WINDOW * P], BF16) for b in range(2)]
        parts = [sb(f"parts{b}", [P, TILES, 3, FEAT], BF16) for b in range(2)]
        prod = [sb(f"prod{b}", [P, max(h * c for h, c in zip(HALF_TILES, PROD_COLS))]) for b in range(2)]
        q_s = sb("q_s", [P, TILES, 2 * MUL])
        q_v = sb("q_v", [P, TILES, 3, 2 * MUL])
        q_v0 = q_v[:].rearrange("p t m c -> p (t m c)")[:, 0:TILES * 3 * MUL].rearrange(
            "p (t m i) -> p t m i", t=TILES, m=3)
        t_a = sb("t_a", [P, TILES, 3 * MUL])
        t_b = sb("t_b", [P, TILES, 3 * MUL])
        t_c = sb("t_c", [P, TILES, 3 * MUL])
        sums = sb("sums", [P, TILES, max(SUM_COLS)])
        msg = sb("msg", [P, TILES, FEAT])
        rest = sb("rest", [P, TILES, FEAT])
        rest2 = sb("rest2", [P, TILES, FEAT])

        wps = psum("wps", [P, 4 * 512])
        hps = psum("hps", [HID, CHUNK])
        acc = [psum(f"acc{g}", [P, 512]) for g in range(GROUPS)]

        loaded = {n: sem(f"{n}_loaded") for n in
                  ("dst_rows", "rel", "nodes", "self", "weights", "l1_weights", "starts", "offs")}
        windows_stored = sem("windows_stored")
        y_stored = sem("y_stored")
        windows_known = sem("windows_known")
        spans_reduced = sem("spans_reduced")
        spans_known = sem("spans_known")
        consts_ready = sem("consts_ready")
        iota_ready = sem("iota_ready")
        self_ready = sem("self_ready")
        self_added = sem("self_added")
        lengths_squared = sem("lengths_squared")
        lengths_ready = sem("lengths_ready")
        y_ready = sem("y_ready")
        w2_scaled = sem("w2_scaled")
        var_ready = sem("var_ready")
        std_ready = sem("std_ready")
        nodes_ready = sem("nodes_ready")
        x1_stored = sem("x1_stored")
        out_stored = sem("out_stored")
        setup_steps = sem("setup_steps")
        gather_turns = sem("gather_turns")
        windows_moved = sem("windows_moved")

        def ring(name):
            return [sem(f"{name}{z}") for z in range(RING)]

        class LayerSemaphores:
            def __init__(self, n):
                self.src_loaded = ring(f"l{n}_src_loaded")
                self.dst_loaded = ring(f"l{n}_dst_loaded")
                self.geo_loaded = ring(f"l{n}_geo_loaded")
                self.mlp_loaded = ring(f"l{n}_mlp_loaded")
                self.rows_gathered = ring(f"l{n}_rows_gathered")
                self.rows_used = ring(f"l{n}_rows_used")
                self.dst_used = ring(f"l{n}_dst_used")
                self.hidden_summed = ring(f"l{n}_hidden_summed")
                self.hidden_ready = ring(f"l{n}_hidden_ready")
                self.weights_ready = sem(f"l{n}_weights_ready")
                self.weights_used = sem(f"l{n}_weights_used")
                self.onehot_ready = sem(f"l{n}_onehot_ready")
                self.parts_ready = sem(f"l{n}_parts_ready")
                self.scattered = sem(f"l{n}_scattered")
                self.acc_added = sem(f"l{n}_acc_added")
                self.act_steps = sem(f"l{n}_act_steps")
                self.dve_steps = sem(f"l{n}_dve_steps")

        layers = [LayerSemaphores(0), LayerSemaphores(1)]

        block = ctx.enter_context(nc.Block())

        def passes(eng):
            eng.wait_ge(windows_known, 1)
            return eng.value_load(passes_i[0:1, 0:1], min_val=1, max_val=PASSES_ALL)

        @block.sync
        def _(sp):
            sp.dma_start(dst_i[:], dst_rows).then_inc(loaded["dst_rows"], 16)
            sp.dma_start(rel_sb[:], rel).then_inc(loaded["rel"], 16)
            sp.dma_start(xs[:], x_self).then_inc(loaded["self"], 16)
            sp.dma_start(si_sb[:], si).then_inc(loaded["self"], 16)
            sp.dma_start(table[:], x_nodes).then_inc(loaded["nodes"], 16)
            sp.dma_start(w1_sb[:], w1_0).then_inc(loaded["weights"], 16)
            sp.dma_start(b1_sb[:, 0:1], b1_0).then_inc(loaded["weights"], 16)
            sp.dma_start(w2_sb[0][:], w2_0).then_inc(loaded["weights"], 16)
            sp.dma_start(w1c_sb[:], w1_1).then_inc(loaded["l1_weights"], 16)
            sp.dma_start(b1_sb[:, 1:2], b1_1).then_inc(loaded["l1_weights"], 16)
            sp.dma_start(w2_sb[1][:], w2_1).then_inc(loaded["l1_weights"], 16)
            sp.wait_ge(windows_known, 1)
            sp.dma_start(lo_dram.rearrange("(r c) -> r c", c=4), lo_f[:]).then_inc(windows_stored, 16)
            sp.dma_start(off_dram.rearrange("(r c) -> r c", c=4), off_i[:]).then_inc(windows_stored, 16)
            sp.wait_ge(windows_stored, 32)
            sp.dma_start(starts[:], lo_dram.unsqueeze(0).broadcast_to([P, N_GROUPS])).then_inc(loaded["starts"], 16)
            sp.dma_start(offs[:, GROUPS:], off_dram.unsqueeze(0)).then_inc(loaded["offs"], 16)
            sp.wait_ge(y_ready, 1)
            sp.dma_start(y_dram, y_all[:].rearrange("p t c -> p (t c)")).then_inc(y_stored, 16)
            sp.wait_ge(y_stored, 16)

            def load_mlp(n, k, z, times):
                s = layers[n]
                if n == 0:
                    sp.wait_ge(s.hidden_summed[z], times)
                    sp.dma_start(mlp_sb[z][:, 0:CHUNK // 4],
                                 feat[bass.ds(k, 1)].rearrange("k p c -> p (k c)")).then_inc(s.mlp_loaded[z], 16)
                else:
                    sp.wait_ge(s.hidden_ready[z], times)
                    sp.dma_start(mlp_sb[z][0:HID, :],
                                 dist[bass.ds(k, 1), :].broadcast_to([HID, CHUNK])).then_inc(s.mlp_loaded[z], 16)

            def stream(n, count):
                s = layers[n]
                if n == 1:
                    sp.wait_ge(x1_stored, 16)
                with sp.Fori(0, count) as j:
                    with sp.Fori(0, ROUNDS) as i:
                        for z in range(RING):
                            k = i * RING + z
                            u = j * ROUNDS + i
                            sp.wait_ge(s.rows_gathered[z], u * (16 * TILES))
                            sp.dma_start(src_sb[z][:], src[bass.ds(k, 1)].rearrange("k p t -> p (k t)")
                                         ).then_inc(s.src_loaded[z], 16)
                            load_mlp(n, k, z, j * MLP_USES[z] + i)
                            sp.wait_ge(s.dst_used[z], u)
                            sp.dma_start(dst_sb[z][:], dst[bass.ds(k, 1)].rearrange("k p t -> p (k t)")
                                         ).then_inc(s.dst_loaded[z], 16)
                            sp.wait_ge(s.rows_used[z], u)
                            if n == 0:
                                sp.dma_start(geo_sb[z][:, :, 0:4], sh[bass.ds(k, 1)].rearrange("k p t c -> p (k t) c")
                                             ).then_inc(s.geo_loaded[z], 16)
                            else:
                                sp.dma_start(geo_sb[z][:].rearrange("p t c -> p (t c)"),
                                             y_dram[:, bass.ds(k * (TILES * 5), TILES * 5)]
                                             ).then_inc(s.geo_loaded[z], 16)
                    load_mlp(n, CHUNKS, 0, j * (ROUNDS + 1) + ROUNDS)

            count = passes(sp)
            stream(0, count)
            sp.wait_ge(nodes_ready, 1)
            sp.dma_start(x1.rearrange("(b p) f -> p b f", p=P), table[:]).then_inc(x1_stored, 16)
            sp.dma_start(starts[:], lo_dram.unsqueeze(0).broadcast_to([P, N_GROUPS])).then_inc(loaded["starts"], 16)
            sp.dma_start(offs[:, GROUPS:], off_dram.unsqueeze(0)).then_inc(loaded["offs"], 16)
            stream(1, count)
            sp.wait_ge(nodes_ready, 2)
            whole = N_NODES // P
            sp.dma_start(out[0:whole * P, :].rearrange("(b p) f -> p b f", p=P), table[:, 0:whole, :]
                         ).then_inc(out_stored, 16)
            sp.dma_start(out[whole * P:, :], table[0:N_NODES - whole * P, whole, :]).then_inc(out_stored, 16)
            sp.wait_ge(out_stored, 32)

        @block.gpsimd
        def _(pool):
            nc.gpsimd.iota(iota[:], pattern=[[1, WINDOW * P]], base=0, channel_multiplier=0,
                           allow_small_or_imprecise_dtypes=True).then_inc(iota_ready, 1)
            pool.wait_ge(spans_reduced, 1)
            nc.gpsimd.partition_all_reduce(span_max[:, 1:2], span_max[:, 0:1], DST_ROWS,
                                           bass.bass_isa.ReduceOp.max).then_inc(spans_known, 1)

            def gather(n, count):
                s = layers[n]
                table_rows = x if n == 0 else x1
                if n == 1:
                    pool.wait_ge(x1_stored, 16)
                with pool.Fori(0, count) as j:
                    with pool.Fori(0, ROUNDS) as i:
                        for z in range(RING):
                            pool.wait_ge(s.rows_used[z], j * ROUNDS + i)
                            pool.wait_ge(s.src_loaded[z], (j * ROUNDS + i) * 16 + 16)
                            pool.sem_inc(gather_turns, 1)
                            for t in range(TILES):
                                nc.gpsimd.indirect_dma_start(
                                    out=rows[z][:, t, :], out_offset=None, in_=table_rows,
                                    in_offset=bass.IndirectOffsetOnAxis(ap=src_sb[z][:, t:t + 1], axis=0),
                                ).then_inc(s.rows_gathered[z], 16)

            count = passes(pool)
            gather(0, count)
            gather(1, count)

        @block.scalar
        def _(act):
            act.wait_ge(lengths_squared, 1)
            work_n = work[:, 0:CHUNKS * TILES]
            nc.scalar.activation(work_n, work_n, ACT.Sqrt).then_inc(lengths_ready, 1)

            def hide(n, j, k, z, round_, first):
                s = layers[n]
                h = hidden[k % 2 if isinstance(k, int) else z % 2]
                if not first:
                    act.wait_ge(s.weights_ready, j * HALVES_READY[n] + (k - 1) * HALVES[n])
                if n == 0:
                    act.wait_ge(s.hidden_summed[z], j * MLP_USES[z] + round_ + 1)
                    nc.scalar.activation(h[0:HID, 0:512], hps[:, 0:512], ACT.Relu, bias=b1_sb[:, 0:1])
                    nc.scalar.activation(h[0:HID, 512:CHUNK], hps[:, 512:CHUNK], ACT.Relu, bias=b1_sb[:, 0:1]
                                         ).then_inc(s.hidden_ready[z], 1)
                else:
                    act.wait_ge(s.mlp_loaded[z], (j * MLP_USES[z] + round_) * 16 + 16)
                    nc.scalar.activation(h[0:HID, :], mlp_sb[z][0:HID, :], ACT.Relu, bias=b1_sb[:, 1:2],
                                         scale=w1c_sb[:, 0:1]).then_inc(s.hidden_ready[z], 1)

            def one_hots(n, j, i, z, steps):
                s = layers[n]
                b = z % 2
                k = i * RING + z
                act.wait_ge(s.dst_loaded[z], (j * ROUNDS + i) * 16 + 16)
                for g in range(GROUPS):
                    t0 = g * GROUP_TILES
                    ins = nc.scalar.activation(ndst[b][:, t0:t0 + GROUP_TILES], dst_sb[z][:, t0:t0 + GROUP_TILES],
                                               ACT.Identity, scale=-1.0,
                                               bias=starts[:, bass.ds(k * GROUPS + g, 1)])
                    steps.done(ins)
                steps.need(steps.n)
                act.nop().then_inc(s.dst_used[z], 1)
                act.wait_ge(s.scattered, j * SCATTERS + k * GROUPS)
                for g in range(GROUPS):
                    for t in range(GROUP_TILES):
                        tt = g * GROUP_TILES + t
                        ins = nc.scalar.activation(gap[g][:, t, :], iota[:], ACT.Abs, bias=ndst[b][:, tt:tt + 1])
                    steps.done(ins)
                for g in range(GROUPS):
                    t0 = g * GROUP_TILES
                    steps.need(steps.n - GROUPS + 1 + g)
                    ins = nc.scalar.activation(onehot[b][:, t0:t0 + GROUP_TILES, :], gap[g][:], ACT.Relu,
                                               scale=-1.0, bias=1.0)
                ins.then_inc(s.onehot_ready, 1)

            def loop(n, count):
                s = layers[n]
                per_round = RING * 2 * GROUPS
                with act.Fori(0, count) as j:
                    act.wait_ge(windows_moved, (0 if n == 0 else count) + j)
                    hide(n, j, 0, 0, 0, True)
                    with act.Fori(0, ROUNDS) as i:
                        steps = Steps(act, s.act_steps, (j * ROUNDS + i) * per_round)
                        for z in range(RING):
                            z1 = (z + 1) % RING
                            hide(n, j, i * RING + z + 1, z1, i + (z + 1) // RING, False)
                            one_hots(n, j, i, z, steps)
                        assert steps.n == per_round
                    act.wait_ge(s.weights_ready, j * HALVES_READY[n] + HALVES_READY[n])

            def deviations(n):
                act.wait_ge(var_ready, n + 1)
                nc.scalar.activation(node_b[:], node_a[:], ACT.Sqrt, scale=1.0 / FEAT, bias=eps[:, 0:1]
                                     ).then_inc(std_ready, 1)

            act.wait_ge(loaded["weights"], 48)
            act.wait_ge(loaded["l1_weights"], 48)
            act.wait_ge(loaded["starts"], 16)
            act.wait_ge(iota_ready, 1)
            act.wait_ge(consts_ready, 1)
            count = passes(act)
            loop(0, count)
            deviations(0)
            act.wait_ge(loaded["starts"], 32)
            loop(1, count)
            deviations(1)

        @block.tensor
        def _(pe):
            pe.wait_ge(loaded["self"], 32)
            for r in range(-(-SELF_CHUNKS // 4)):
                if r >= 4:
                    pe.wait_ge(self_added, r - 3)
                for c in range(4 * r, min(4 * r + 4, SELF_CHUNKS)):
                    col = (r % 4) * 512 + (c % 4) * P
                    ins = nc.tensor.matmul(wps[:, col:col + P], xs[:, c, :], si_sb[:], start=True, stop=True)
                ins.then_inc(self_ready, 1)
            pe.wait_ge(self_added, -(-SELF_CHUNKS // 4))

            def weigh(n, j, k, z, round_, first):
                s = layers[n]
                if n == 0:
                    pe.wait_ge(s.mlp_loaded[z], (j * MLP_USES[z] + round_) * 16 + 16)
                    if not first:
                        zp = (z - 1) % RING
                        pe.wait_ge(s.hidden_ready[zp], j * MLP_USES[zp] + round_ + (0 if z == 0 else 1))
                    for c in range(4):
                        ins = nc.tensor.matmul(hps[:, c * 256:(c + 1) * 256], w1_sb[:, c, :], mlp_sb[z][:, 0:256],
                                               start=True, stop=True)
                    ins.then_inc(s.hidden_summed[z], 1)
                pe.wait_ge(s.hidden_ready[z], j * MLP_USES[z] + round_ + 1)
                weigh_halves(n, j, k, z, (0, 1), first)

            def weigh_halves(n, j, k, z, halves, first=False):
                s = layers[n]
                for q in halves:
                    if not first:
                        pe.wait_ge(s.weights_used, (j * CHUNKS + k) * HALVES[n] + (q - 1))
                    for t in range(HALF_TILES[n]):
                        col = (q % 2) * 1024 + t * (1024 // HALF_TILES[n])
                        e0 = (q * HALF_TILES[n] + t) * P
                        ins = nc.tensor.matmul(wps[:, col:col + W_COLS[n]], hidden[z % 2][:, e0:e0 + P], w2_sb[n][:],
                                               start=True, stop=True)
                    ins.then_inc(s.weights_ready, 1)

            def scatter(n, j, i, z):
                s = layers[n]
                k = i * RING + z
                b = z % 2
                pe.wait_ge(s.onehot_ready, j * CHUNKS + k + 1)
                pe.wait_ge(s.parts_ready, j * CHUNKS + k + 1)
                for g in range(GROUPS):
                    pe.wait_ge(s.acc_added, j * SCATTERS + k * GROUPS + g + 1)
                    for w in range(WINDOW):
                        for t in range(GROUP_TILES):
                            for part in range(3):
                                tt = g * GROUP_TILES + t
                                ins = nc.tensor.matmul(acc[g][:, w * FEAT:(w + 1) * FEAT],
                                                       onehot[b][:, tt, w * P:(w + 1) * P], parts[b][:, tt, part, :],
                                                       start=(t == 0 and part == 0),
                                                       stop=(t == GROUP_TILES - 1 and part == 2))
                    ins.then_inc(s.scattered, 1)

            def loop(n, count):
                s = layers[n]
                with pe.Fori(0, count) as j:
                    pe.wait_ge(s.acc_added, j * SCATTERS)
                    for g in range(GROUPS):
                        nc.tensor.matmul(acc[g][:, 0:WINDOW * FEAT], zeros[:], zeros[:, 0:WINDOW * FEAT],
                                         start=True, stop=True).then_inc(s.scattered, 1)
                    weigh(n, j, 0, 0, 0, True)
                    with pe.Fori(0, ROUNDS) as i:
                        for z in range(RING):
                            z1 = (z + 1) % RING
                            weigh_halves(n, j, i * RING + z, z, range(2, HALVES[n]))
                            weigh(n, j, i * RING + z + 1, z1, i + (z + 1) // RING, False)
                            scatter(n, j, i, z)

            pe.wait_ge(loaded["weights"], 48)
            pe.wait_ge(consts_ready, 1)
            pe.wait_ge(w2_scaled, 1)
            count = passes(pe)
            loop(0, count)
            pe.wait_ge(nodes_ready, 1)
            loop(1, count)

        @block.vector
        def _(dve):
            st = Steps(dve, setup_steps)

            def chain(instruction):
                st.need(st.done(instruction))

            for b in range(2):
                st.done(nc.vector.memset(hidden[b][HID:P, :], 0.0))
            st.done(nc.vector.memset(zeros[:], 0.0))
            st.done(nc.vector.memset(eps[:], LN_EPS))
            st.done(nc.vector.memset(offs[:, 0:GROUPS], 0))
            st.need(st.n)
            for b in range(2):
                chain(nc.vector.memset(hidden[b][HID:HID + 1, :], 1.0))

            dve.wait_ge(loaded["dst_rows"], 16)
            blk = work[0:DST_ROWS, 0:4 * GROUP]
            pad = work[0:DST_ROWS, 4 * GROUP:8 * GROUP]
            chain(nc.vector.tensor_single_scalar(dst_i[:], dst_i[:], 7, ALU.arith_shift_right))
            chain(nc.vector.tensor_copy(blk, dst_i[:]))
            st.done(nc.vector.tensor_scalar(pad, blk, 0.0, float(2 * BLOCKS), ALU.is_lt, ALU.mult))
            chain(nc.vector.tensor_reduce(highest[:], blk.rearrange("r (g e) -> r g e", g=4), AX_X, ALU.max))
            chain(nc.vector.tensor_tensor(blk, blk, pad, ALU.add))
            chain(nc.vector.tensor_reduce(lowest[:], blk.rearrange("r (g e) -> r g e", g=4), AX_X, ALU.min))
            chain(nc.vector.tensor_tensor(span[:], highest[:], lowest[:], ALU.subtract))
            nc.vector.tensor_reduce(span_max[:, 0:1], span[:], AX_X, ALU.max).then_inc(spans_reduced, 1)
            chain(nc.vector.tensor_scalar(lowest[:], lowest[:], float(BLOCKS - WINDOW), None, ALU.min))
            dve.wait_ge(spans_known, 1)
            chain(nc.vector.tensor_scalar(fits[:], span_max[:, 1:2], float(WINDOW) - 0.5, None, ALU.is_lt))
            chain(nc.vector.tensor_scalar(passes_f[:], fits[:], float(1 - PASSES_ALL), float(PASSES_ALL),
                                          ALU.mult, ALU.add))
            chain(nc.vector.tensor_copy(passes_i[:], passes_f[:]))
            chain(nc.vector.tensor_scalar(lo_f[:], lowest[:], fits[:, 0:1], float(P), ALU.mult, ALU.mult))
            chain(nc.vector.tensor_scalar(off_f[:], lowest[:], fits[:, 0:1], float(FEAT), ALU.mult, ALU.mult))
            chain(nc.vector.tensor_copy(off_i[:], off_f[:]))
            dve.nop().then_inc(windows_known, 1)

            dve.wait_ge(loaded["rel"], 16)
            sq = work[:, 0:CHUNKS * TILES * 3].rearrange("p (t c) -> p t c", c=3)
            chain(nc.vector.tensor_tensor(sq, rel_sb[:], rel_sb[:], ALU.mult))
            chain(nc.vector.tensor_reduce(y_all[:, :, 0:1].rearrange("p t c -> p (t c)"), sq, AX_X, ALU.add))
            nc.vector.tensor_copy(work[:, 0:CHUNKS * TILES], y_all[:, :, 0:1].rearrange("p t c -> p (t c)")
                                  ).then_inc(lengths_squared, 1)
            dve.wait_ge(lengths_ready, 1)
            length = work[:, 0:CHUNKS * TILES]
            inv = work[:, CHUNKS * TILES:2 * CHUNKS * TILES]
            chain(nc.vector.reciprocal(inv, length))
            st.done(nc.vector.tensor_tensor(y_all[:, :, 0:2], rel_sb[:, :, 1:3],
                                            inv.unsqueeze(2).broadcast_to([P, CHUNKS * TILES, 2]), ALU.mult))
            chain(nc.vector.tensor_tensor(y_all[:, :, 2:5], rel_sb[:],
                                          inv.unsqueeze(2).broadcast_to([P, CHUNKS * TILES, 3]), ALU.mult))
            dve.nop().then_inc(y_ready, 1)

            dve.wait_ge(loaded["weights"], 48)
            v0 = w2_sb[0][:, 0:128].rearrange("p (o a i) -> p o a i", a=2, i=MUL)
            chain(nc.vector.tensor_scalar(w2_sb[0][:], w2_sb[0][:], ALPHA, None, ALU.mult))
            st.done(nc.vector.tensor_scalar(v0[:, :, 1, :], v0[:, :, 1, :], C110, None, ALU.mult))
            dve.wait_ge(loaded["l1_weights"], 48)
            ab = w2_sb[1][:, 0:128].rearrange("p (o a i) -> p o a i", a=2, i=MUL)
            cd = w2_sb[1][:, 128:256].rearrange("p (o a i) -> p o a i", a=2, i=MUL)
            ef = w2_sb[1][:, 256:384].rearrange("p (o a i) -> p o a i", a=2, i=MUL)
            st.done(nc.vector.tensor_scalar(ab[:, :, 0, :], ab[:, :, 0, :], K_00, None, ALU.mult))
            st.done(nc.vector.tensor_scalar(ab[:, :, 1, :], ab[:, :, 1, :], K_01, None, ALU.mult))
            st.done(nc.vector.tensor_scalar(cd[:, :, 0, :], cd[:, :, 0, :], K_10, None, ALU.mult))
            st.done(nc.vector.tensor_scalar(ef[:, :, 1, :], ef[:, :, 1, :], K_11_1, None, ALU.mult))
            chain(nc.vector.tensor_scalar(cd[:, :, 1, :], cd[:, :, 1, :], K_11_2, None, ALU.mult))
            chain(nc.vector.tensor_scalar(w2_tmp[:], cd[:, :, 1, :], -1.0 / 3.0, None, ALU.mult))
            chain(nc.vector.scalar_tensor_tensor(out=ef[:, :, 0, :], in0=ef[:, :, 0, :], scalar=K_11_0, in1=w2_tmp[:],
                                                 op0=ALU.mult, op1=ALU.add))
            dve.nop().then_inc(w2_scaled, 1)

            dve.wait_ge(loaded["nodes"], 16)
            for r in range(-(-SELF_CHUNKS // 4)):
                dve.wait_ge(self_ready, r + 1)
                b0, b1 = 16 * r, min(16 * r + 16, BLOCKS)
                chain(nc.vector.scalar_tensor_tensor(
                    out=table[:, b0:b1, :],
                    in0=wps[:, (r % 4) * 512:(r % 4) * 512 + (b1 - b0) * FEAT].rearrange("p (b f) -> p b f", f=FEAT),
                    scalar=SI_SCALE, in1=table[:, b0:b1, :], op0=ALU.mult, op1=ALU.add))
                dve.nop().then_inc(self_added, 1)
            dve.nop().then_inc(consts_ready, 1)
            dve.wait_ge(loaded["offs"], 16)
            dve.wait_ge(loaded["starts"], 16)

            def add_sums(n, j, k):
                s = layers[n]
                flat = table[:].rearrange("p b f -> p (b f)")
                cols = [dve.value_load(offs[0:1, bass.ds(k * GROUPS + g, 1)], min_val=0,
                                       max_val=(BLOCKS - WINDOW) * FEAT) for g in range(GROUPS)]
                for g in range(GROUPS):
                    dve.wait_ge(s.scattered, j * SCATTERS + k * GROUPS + g + 1)
                    window = flat[:, bass.ds(cols[g], WINDOW * FEAT)]
                    ins = nc.vector.tensor_tensor(window, window, acc[g][:, 0:WINDOW * FEAT], ALU.add)
                    ins.then_inc(s.acc_added, 1)
                    dve.wait_ge(s.acc_added, j * SCATTERS + k * GROUPS + g + 1)

            def vec_im(ap):
                return ap.rearrange("p t (i m) -> p t i m", m=3)

            def vec_mi(ap):
                return ap.rearrange("p t (i m) -> p t m i", m=3)

            def prepare0(r, geo, steps):
                s_, v_ = r[:, :, 0:MUL], r[:, :, MUL:FEAT]
                sh0 = geo[:, :, 0:1]
                a = steps.done(nc.vector.tensor_tensor(
                    vec_im(t_a[:]), vec_im(v_), geo[:, :, 1:4].unsqueeze(2).broadcast_to([P, TILES, MUL, 3]), ALU.mult))
                steps.done(nc.vector.tensor_tensor(q_s[:, :, 0:MUL], s_, sh0.broadcast_to([P, TILES, MUL]), ALU.mult))
                steps.done(nc.vector.tensor_tensor(
                    q_v0, vec_mi(v_),
                    sh0.unsqueeze(3).broadcast_to([P, TILES, 3, MUL]), ALU.mult))
                steps.need(a)
                return steps.done(nc.vector.tensor_reduce(q_s[:, :, MUL:2 * MUL], vec_im(t_a[:]), AX_X, ALU.add))

            def prepare1(r, geo, steps):
                s_, v_ = r[:, :, 0:MUL], r[:, :, MUL:FEAT]
                a = steps.done(nc.vector.tensor_tensor(
                    vec_im(t_a[:]), vec_im(v_), geo[:, :, 0:3].unsqueeze(2).broadcast_to([P, TILES, MUL, 3]), ALU.mult))
                steps.done(nc.vector.tensor_copy(q_v[:, :, :, 0:MUL], vec_mi(v_)))
                steps.done(nc.vector.tensor_copy(q_s[:, :, 0:MUL], s_))
                vm = vec_mi(v_)

                def y_times_v(out, y0, m0, count):
                    return steps.done(nc.vector.tensor_tensor(
                        out, vm[:, :, m0:m0 + count, :],
                        geo[:, :, y0:y0 + count].unsqueeze(3).broadcast_to([P, TILES, count, MUL]), ALU.mult))

                left = t_b[:].rearrange("p t (m i) -> p t m i", m=3)
                right = t_c[:].rearrange("p t (m i) -> p t m i", m=3)
                y_times_v(left[:, :, 0:1, :], 1, 2, 1)
                y_times_v(left[:, :, 1:3, :], 2, 0, 2)
                y_times_v(right[:, :, 0:2, :], 2, 1, 2)
                c = y_times_v(right[:, :, 2:3, :], 4, 0, 1)
                steps.need(a)
                steps.done(nc.vector.tensor_reduce(q_s[:, :, MUL:2 * MUL], vec_im(t_a[:]), AX_X, ALU.add))
                steps.need(c)
                return steps.done(nc.vector.tensor_tensor(q_v[:, :, :, MUL:2 * MUL], left, right, ALU.subtract))

            def multiply0(q, r, steps):
                T = HALF_TILES[0]
                t0 = q * T
                w = wps[:, (q % 2) * 1024:(q % 2) * 1024 + 1024].rearrange("p (t c) -> p t c", t=T)
                pr = prod[q % 2][:, 0:T * PROD_COLS[0]].rearrange("p (t c) -> p t c", t=T)
                nc.vector.tensor_tensor(
                    pr[:, :, 0:128].rearrange("p t (o c) -> p t o c", o=MUL),
                    w[:, :, 0:128].rearrange("p t (o c) -> p t o c", o=MUL),
                    q_s[:, t0:t0 + T, :].unsqueeze(2).broadcast_to([P, T, MUL, 2 * MUL]), ALU.mult)
                nc.vector.tensor_tensor(
                    pr[:, :, 128:192].rearrange("p t (o i) -> p t o i", o=MUL),
                    w[:, :, 128:192].rearrange("p t (o i) -> p t o i", o=MUL),
                    r[:, t0:t0 + T, 0:MUL].unsqueeze(2).broadcast_to([P, T, MUL, MUL]), ALU.mult)
                return nc.vector.tensor_tensor(
                    pr[:, :, 192:384].rearrange("p t (m o i) -> p t m o i", m=3, o=MUL),
                    w[:, :, 192:256].rearrange("p t (o i) -> p t o i", o=MUL).unsqueeze(2)
                    .broadcast_to([P, T, 3, MUL, MUL]),
                    q_v0[:, t0:t0 + T].unsqueeze(3).broadcast_to([P, T, 3, MUL, MUL]), ALU.mult)

            def multiply1(q, r, steps):
                T = HALF_TILES[1]
                t0 = q * T
                C = 2 * MUL
                w = wps[:, (q % 2) * 1024:(q % 2) * 1024 + 1024].rearrange("p (t c) -> p t c", t=T)
                pr = prod[q % 2][:, 0:T * PROD_COLS[1]].rearrange("p (t c) -> p t c", t=T)
                nc.vector.tensor_tensor(
                    pr[:, :, 0:256].rearrange("p t (o c) -> p t o c", c=C),
                    w[:, :, 0:256].rearrange("p t (o c) -> p t o c", c=C),
                    q_s[:, t0:t0 + T, :].unsqueeze(2).broadcast_to([P, T, C, C]), ALU.mult)
                return nc.vector.tensor_tensor(
                    pr[:, :, 256:640].rearrange("p t (m o c) -> p t m o c", m=3, c=C),
                    w[:, :, 256:384].rearrange("p t (o c) -> p t o c", c=C).unsqueeze(2)
                    .broadcast_to([P, T, 3, MUL, C]),
                    q_v[:, t0:t0 + T].unsqueeze(3).broadcast_to([P, T, 3, MUL, C]), ALU.mult)

            def messages(n, j, i, z, steps):
                s = layers[n]
                k = i * RING + z
                r, geo = rows[z], geo_sb[z]
                T, H = HALF_TILES[n], HALVES[n]
                dve.wait_ge(s.rows_gathered[z], (j * ROUNDS + i) * (16 * TILES) + 16 * TILES)
                dve.wait_ge(s.geo_loaded[z], (j * ROUNDS + i) * 16 + 16)
                steps.need((prepare0, prepare1)[n](r, geo, steps))
                inner = MUL if n == 0 else 2 * MUL

                def reduce(q):
                    pr = prod[q % 2][:, 0:T * PROD_COLS[n]].rearrange("p (t o c) -> p t o c", t=T, c=inner)
                    dve.wait_ge(s.weights_used, (j * CHUNKS + k) * H + q + 1)
                    return steps.done(nc.vector.tensor_reduce(sums[:, q * T:(q + 1) * T, 0:SUM_COLS[n]], pr,
                                                              AX_X, ALU.add))

                for q in range(H):
                    dve.wait_ge(s.weights_ready, j * HALVES_READY[n] + k * H + q + 1)
                    (multiply0, multiply1)[n](q, r, steps).then_inc(s.weights_used, 1)
                    if q == 0:
                        add_sums(n, j, k)
                    last = reduce(q)
                steps.need(last)
                scale = geo[:, :, 1:4] if n == 0 else geo[:, :, 0:3]
                along = sums[:, :, 2 * MUL:3 * MUL] if n == 0 else sums[:, :, MUL:2 * MUL]
                vec0 = 3 * MUL if n == 0 else 2 * MUL
                a = steps.done(nc.vector.tensor_tensor(
                    vec_im(t_a[:]), along.unsqueeze(3).broadcast_to([P, TILES, MUL, 3]),
                    scale.unsqueeze(2).broadcast_to([P, TILES, MUL, 3]), ALU.mult))
                if n == 0:
                    pair = sums[:, :, 0:2 * MUL].rearrange("p t (o a) -> p t o a", a=2)
                    steps.done(nc.vector.tensor_tensor(msg[:, :, 0:MUL], pair[:, :, :, 0], pair[:, :, :, 1], ALU.add))
                else:
                    steps.done(nc.vector.tensor_copy(msg[:, :, 0:MUL], sums[:, :, 0:MUL]))
                steps.need(a)
                m = steps.done(nc.vector.tensor_tensor(
                    vec_im(msg[:, :, MUL:FEAT]), vec_im(t_a[:]),
                    sums[:, :, vec0:vec0 + 3 * MUL].rearrange("p t (m o) -> p t o m", m=3), ALU.add))
                steps.need(m)
                dve.nop().then_inc(s.rows_used[z], 1)
                pt = parts[z % 2]
                dve.wait_ge(s.scattered, j * SCATTERS + k * GROUPS)
                steps.need(steps.done(nc.vector.tensor_copy(pt[:, :, 0, :], msg[:])))
                steps.need(steps.done(nc.vector.tensor_tensor(rest[:], msg[:], pt[:, :, 0, :], ALU.subtract)))
                steps.need(steps.done(nc.vector.tensor_copy(pt[:, :, 1, :], rest[:])))
                nc.vector.tensor_tensor(pt[:, :, 2, :], rest[:], pt[:, :, 1, :], ALU.subtract
                                        ).then_inc(s.parts_ready, 1)

            def loop(n, count):
                s = layers[n]
                per_chunk = ((4, 9)[n] + HALVES[n] + 3 + 3)
                with dve.Fori(0, count) as j:
                    with dve.Fori(0, ROUNDS) as i:
                        steps = Steps(dve, s.dve_steps, (j * ROUNDS + i) * (RING * per_chunk))
                        for z in range(RING):
                            messages(n, j, i, z, steps)
                        assert steps.n == RING * per_chunk, steps.n
                    add_sums(n, j, CHUNKS)
                    dve.wait_ge(s.onehot_ready, j * CHUNKS + CHUNKS)
                    nc.vector.tensor_scalar(offs[:], offs[:], WINDOW * FEAT, None, ALU.add)
                    nc.vector.tensor_scalar(starts[:], starts[:], float(WINDOW * P), None, ALU.add
                                            ).then_inc(windows_moved, 1)
                    dve.wait_ge(windows_moved, (0 if n == 0 else count) + j + 1)

            def normalize(n):
                sq_ = work[:, 0:BLOCKS * FEAT].rearrange("p (b f) -> p b f", f=FEAT)
                chain(nc.vector.tensor_reduce(node_a[:], table[:], AX_X, ALU.add))
                chain(nc.vector.tensor_scalar(node_c[:], node_a[:], 1.0 / FEAT, None, ALU.mult))
                chain(nc.vector.tensor_tensor(table[:], table[:], node_c[:].unsqueeze(2).broadcast_to([P, BLOCKS, FEAT]),
                                              ALU.subtract))
                chain(nc.vector.tensor_tensor(sq_, table[:], table[:], ALU.mult))
                nc.vector.tensor_reduce(node_a[:], sq_, AX_X, ALU.add).then_inc(var_ready, 1)
                dve.wait_ge(std_ready, n + 1)
                chain(nc.vector.reciprocal(node_c[:], node_b[:]))
                nc.vector.tensor_tensor(table[:], table[:], node_c[:].unsqueeze(2).broadcast_to([P, BLOCKS, FEAT]),
                                        ALU.mult).then_inc(nodes_ready, 1)

            count = passes(dve)
            loop(0, count)
            normalize(0)
            dve.wait_ge(x1_stored, 16)
            dve.wait_ge(loaded["offs"], 32)
            dve.wait_ge(loaded["starts"], 32)
            chain(nc.vector.memset(offs[:, 0:GROUPS], 0))
            loop(1, count)
            normalize(1)


_OUT = ((N_NODES, FEAT), "float32")


def kernel(x, src, dst, edge_attr_3, edge_attr_32, edge_attr_4, edge_weight, L0_gnn_W1, L0_gnn_b1, L0_gnn_W2,
           L0_gnn_b2, L0_gnn_si_w0, L0_gnn_si_w1, L1_gnn_w1, L1_gnn_b1, L1_gnn_w2, L1_gnn_b2):
    import concourse.bacc as bacc
    from concourse.bass_utils import run_bass_kernel_spmd

    def padded(a, n, value):
        a = np.asarray(a)
        return np.concatenate([a, np.full((n - a.shape[0], *a.shape[1:]), value, a.dtype)])

    def by_partition(a):
        return np.swapaxes(a.reshape(CHUNKS, TILES, P, *a.shape[1:]), 1, 2)

    x = np.asarray(x)
    x_pad = padded(x, SELF_CHUNKS * 4 * P, 0)
    dst_p = padded(dst, EDGES, -1)
    feat = padded(edge_attr_32, EDGES + AHEAD * CHUNK, 0).reshape(CHUNKS + AHEAD, 4, CHUNK // 4, FEAT)
    rel = by_partition(padded(edge_attr_3, EDGES, 1))
    W1 = np.zeros((4, FEAT, 4, HID), np.float32)
    for s in range(4):
        W1[s, :, s, :] = np.asarray(L0_gnn_W1)
    S = np.zeros((4, FEAT, 4, FEAT), np.float32)
    for b in range(4):
        S[b, :MUL, b, :MUL] = np.asarray(L0_gnn_si_w0)
        for m in range(3):
            S[b, MUL + m::3, b, MUL + m::3] = np.asarray(L0_gnn_si_w1)

    def with_bias(w, b, cols):
        out = np.zeros((P, len(cols)), np.float32)
        out[:HID] = np.asarray(w)[:, cols]
        out[HID] = np.asarray(b)[cols]
        return out

    i, o = np.arange(MUL)[None, :], np.arange(MUL)[:, None]
    mm = MUL * MUL
    col0 = [p * mm + i * MUL + o for p in range(4)]
    cols0 = np.concatenate([np.concatenate([col0[0], col0[3]], 1).ravel(), col0[1].ravel(), col0[2].ravel()])
    uv = o * MUL + i
    col1 = [uv, mm + uv, 2 * mm + uv] + [3 * mm + uv * 3 + l for l in range(3)]
    cols1 = np.concatenate([np.concatenate(c, 1).ravel() for c in
                            ((col1[0], col1[1]), (col1[2], col1[5]), (col1[3], col1[4]))])

    arrays = {
        "x": x,
        "x_nodes": np.swapaxes(x_pad[:BLOCKS * P].reshape(BLOCKS, P, FEAT), 0, 1),
        "x_self": x_pad.reshape(SELF_CHUNKS, 4, P, FEAT).transpose(1, 3, 0, 2).reshape(P, SELF_CHUNKS, P),
        "src": by_partition(padded(src, EDGES, 0)),
        "dst": by_partition(dst_p),
        "dst_rows": dst_p.reshape(DST_ROWS, 4 * GROUP),
        "sh": by_partition(padded(edge_attr_4, EDGES, 0)),
        "feat": np.swapaxes(feat, 2, 3).reshape(CHUNKS + AHEAD, P, CHUNK // 4),
        "rel": np.swapaxes(rel, 0, 1).reshape(P, CHUNKS * TILES, 3),
        "dist": padded(edge_weight, EDGES + AHEAD * CHUNK, 0).reshape(CHUNKS + AHEAD, CHUNK),
        "w1_0": W1.reshape(P, 4, HID),
        "b1_0": np.asarray(L0_gnn_b1).reshape(HID, 1),
        "w2_0": with_bias(L0_gnn_W2, L0_gnn_b2, cols0),
        "si": S.reshape(P, P),
        "w1_1": np.asarray(L1_gnn_w1).reshape(HID, 1),
        "b1_1": np.asarray(L1_gnn_b1).reshape(HID, 1),
        "w2_1": with_bias(L1_gnn_w2, L1_gnn_b2, cols1),
    }
    nc = bacc.Bacc("TRN2", target_bir_lowering=False, num_devices=1)
    args, ins = {}, {}
    for name, a in arrays.items():
        ins[f"in_{name}"] = np.ascontiguousarray(a)
        args[name] = nc.dram_tensor(f"in_{name}", a.shape, mybir.dt.from_np(a.dtype), kind="ExternalInput").ap()
    out = nc.dram_tensor("out_0", _OUT[0], F32, kind="ExternalOutput").ap()
    build(nc, out=out, **args)
    r = run_bass_kernel_spmd(nc, [ins], core_ids=[0])
    return r.results[0]["out_0"]
```

```python
from contextlib import ExitStack
from math import pi, sqrt

import numpy as np

import concourse.bass as bass
from concourse import mybir

F32, BF16, I32 = mybir.dt.float32, mybir.dt.bfloat16, mybir.dt.int32
ALU = mybir.AluOpType
ACT = mybir.ActivationFunctionType
AX_X = mybir.AxisListType.X

P = 128
N_NODES, N_EDGES = 12500, 200000
MUL, FEAT = 8, 32
HID = 64
TILES = 16
CHUNK = TILES * P
RING = 2
CHUNKS = -(-N_EDGES // (CHUNK * RING)) * RING
ROUNDS = CHUNKS // RING
EDGES = CHUNKS * CHUNK
SETS = 4
SET = CHUNK // SETS
GROUP_TILES = 4
GROUPS = TILES // GROUP_TILES
N_GROUPS = CHUNKS * GROUPS
GROUP = GROUP_TILES * P
BLOCKS = -(-N_NODES // P)
PASSES_ALL = BLOCKS
FAR = float(4 * BLOCKS * P)
SELF_CHUNKS = -(-BLOCKS // 4)
LN_EPS = 1e-5

MM = MUL * MUL
W_PATHS, PATHS = (4, 7), (6, 7)
HALF_TILES = (4, 2)
HALVES = tuple(TILES // h for h in HALF_TILES)
PLAN = TILES + 2 * GROUPS
PE_TILES = ((0, 6), (6, 14))
PE_HALVES = tuple(-(-PE_TILES[n][1] // HALF_TILES[n]) for n in range(2))
DVE_SUMS = (((6, 11), (11, 16)), ((0, 6), (14, 16)))
GEO = (4, 9)
FRAME_PARTS = 2
PART_TILES = CHUNKS * TILES // FRAME_PARTS
ALPHA, C110, SI_SCALE = 0.25, 1.0 / sqrt(3.0), 1.0 / sqrt(MUL)
NORM0 = sqrt(4 * pi) / sqrt(2 * MUL)
NORM1 = sqrt(4 * pi) * sqrt(3.0) / sqrt(4 * MUL)
Y0, Y1 = 0.5 / sqrt(pi), sqrt(3.0 / (4 * pi))
K_00 = NORM0 * Y0
K_01 = NORM0 * Y1 / sqrt(3.0)
K_10 = NORM1 * Y1 / sqrt(3.0)
K_11_0 = NORM1 * Y0 / sqrt(3.0)
K_11_1 = NORM1 * Y1 / sqrt(6.0)
K_11_2 = NORM1 * sqrt(3.0 / (8 * pi))


class Steps:

    def __init__(self, eng, sem, base=0):
        self.eng, self.sem, self.base, self.n = eng, sem, base, 0

    def done(self, instruction):
        instruction.then_inc(self.sem, 1)
        self.n += 1
        return self.n

    def need(self, n):
        self.eng.wait_ge(self.sem, self.base + n)


BODY_STEPS, PROLOGUE_STEPS, TAIL_STEPS = (9, 10), (6, 7), (10, 12)


def build(nc, x, x_nodes, x_self, src, dst, dst_rows, sh, feat, rel, dist, identity, w1_0, b1_0, w2_0, si, w1_1, b1_1,
          w2_1, out):
    x1 = nc.dram_tensor("x1_rows", [BLOCKS * P, FEAT], F32).ap()
    frame_dram = nc.dram_tensor("frames", [P, CHUNKS * TILES * GEO[1]], F32).ap()
    off_dram = nc.dram_tensor("window_offsets", [N_GROUPS], I32).ap()
    rem_dram = nc.dram_tensor("window_remainders", [N_GROUPS], F32).ap()

    with ExitStack() as ctx:
        def sb(name, shape, dt=F32):
            return ctx.enter_context(nc.sbuf_tensor(name, shape, dt))

        def psum(name, shape, dt=F32):
            return ctx.enter_context(nc.psum_tensor(name, shape, dt))

        def sem(name):
            return ctx.enter_context(nc.semaphore(name))

        def slots(make):
            return [make(z) for z in range(RING)]

        table = sb("table", [P, BLOCKS + 1, FEAT])
        plan0 = sb("plan0", [P, CHUNKS, PLAN])
        plan = sb("plan", [P, CHUNKS, PLAN])
        offs0 = sb("offs0", [1, GROUPS + N_GROUPS], I32)
        offs = sb("offs", [1, GROUPS + N_GROUPS], I32)
        w1_sb = sb("w1_sb", [P, 2, P])
        b1_sb = sb("b1_sb", [P, 2])
        w1c_sb = sb("w1c_sb", [HID, 1])
        w2_sb = [sb(f"w2_sb{n}", [P, W_PATHS[n], MM]) for n in range(2)]
        ident = sb("ident", [P, P])
        iota = sb("iota", [P, P])
        iota_p = sb("iota_p", [P, 1])
        eps = sb("eps", [P, 1])
        node_a = sb("node_a", [P, BLOCKS])
        node_b = sb("node_b", [P, BLOCKS])
        node_c = sb("node_c", [P, BLOCKS])
        work = sb("work", [P, 8 * GROUP])
        rel_sb = sb("rel_sb", [P, PART_TILES, 3])
        dst_i = sb("dst_i", [P, 4 * GROUP], I32)
        dst_t = sb("dst_t", [P, CHUNKS * TILES], I32)
        rem_sb = sb("rem_sb", [P, N_GROUPS])
        si_sb = sb("si_sb", [P, P])
        w2_tmp = sb("w2_tmp", [P, MM])
        lowest = sb("lowest", [P, 4])
        highest = sb("highest", [P, 4])
        span = sb("span", [P, 4])
        span_max = sb("span_max", [P, 2])
        fits = sb("fits", [P, 1])
        passes_f = sb("passes_f", [P, 1])
        passes_i = sb("passes_i", [P, 1], I32)
        start_i = sb("start_i", [P, 4], I32)
        off_i = sb("off_i", [P, 4], I32)
        rem_i = sb("rem_i", [P, 4], I32)
        rem_f = sb("rem_f", [P, 4])
        src_sb = slots(lambda z: sb(f"src{z}", [P, TILES], I32))
        geo_sb = slots(lambda z: sb(f"geo{z}", [P, TILES * max(GEO)]))
        mlp_sb = slots(lambda z: sb(f"mlp{z}", [P, CHUNK]))
        rows = slots(lambda z: sb(f"rows{z}", [P, TILES, FEAT]))
        hidden = sb("hidden", [P, RING, CHUNK])
        plan_sb = slots(lambda z: sb(f"slot_plan{z}", [P, PLAN]))
        gap = sb("gap", [P, TILES, P], BF16)
        onehot = slots(lambda z: sb(f"onehot{z}", [P, TILES, P], BF16))
        parts = slots(lambda z: sb(f"parts{z}", [P, TILES, 3, FEAT], BF16))
        q_sb = slots(lambda z: sb(f"q{z}", [P, TILES * PATHS[1] * MUL]))
        split = slots(lambda z: sb(f"split{z}", [P, GROUPS, 2 * FEAT]))
        msg = sb("msg", [P, TILES, FEAT])
        rest = sb("rest", [P, TILES, FEAT])
        prod = sb("prod", [P, TILES * PATHS[1] * MM])
        sums = sb("sums", [P, TILES * PATHS[1] * MUL])
        t_a = sb("t_a", [P, TILES * 9 * MUL])
        t_b = sb("t_b", [P, TILES * 9 * MUL])
        xs = hidden[:].rearrange("p b c -> p (b c)")[:, 0:SELF_CHUNKS * P].rearrange("p (s c) -> p s c", c=P)

        wps = psum("wps", [P, 4 * 512])
        hps = psum("hps", [P, SET])
        acc = slots(lambda z: psum(f"acc{z}", [P, 512]))
        red = psum("red", [P, 512])

        loaded = {n: sem(f"{n}_loaded") for n in
                  ("dst_rows", "dst", "rel", "nodes", "self", "weights", "l1_weights", "rem", "offs")}
        windows_stored = sem("windows_stored")
        frames_stored = sem("frames_stored")
        windows_known = sem("windows_known")
        spans_reduced = sem("spans_reduced")
        spans_known = sem("spans_known")
        consts_ready = sem("consts_ready")
        iota_ready = sem("iota_ready")
        self_ready = sem("self_ready")
        self_added = sem("self_added")
        lengths_squared = sem("lengths_squared")
        lengths_ready = sem("lengths_ready")
        rel_used = sem("rel_used")
        frames_ready = sem("frames_ready")
        w2_scaled = sem("w2_scaled")
        var_ready = sem("var_ready")
        std_ready = sem("std_ready")
        nodes_ready = sem("nodes_ready")
        x1_stored = sem("x1_stored")
        out_stored = sem("out_stored")
        setup_steps = sem("setup_steps")
        gather_turns = sem("gather_turns")
        dve_turns = sem("dve_turns")
        windows_moved = sem("windows_moved")

        class LayerSemaphores:

            def __init__(self, n):
                self.per_chunk = []

                def ring(name, count=1):
                    made = slots(lambda z: sem(f"l{n}_{name}{z}"))
                    self.per_chunk += [(semaphore, count) for semaphore in made]
                    return made

                self.src_loaded = ring("src_loaded", 16)
                self.geo_loaded = ring("geo_loaded", 16)
                self.mlp_loaded = ring("mlp_loaded", 16)
                self.rows_gathered = slots(lambda z: sem(f"l{n}_rows_gathered{z}"))
                self.rows_read = ring("rows_read")
                self.rows_copied = ring("rows_copied")
                self.q_completed = ring("q_completed")
                self.geo_used = ring("geo_used")
                self.hidden_summed = ring("hidden_summed", 2)
                self.hidden_ready = ring("hidden_ready", 2)
                self.weights_ready = ring("weights_ready", HALVES[n])
                self.weights_used = ring("weights_used", HALVES[n])
                self.products_summed = ring("products_summed")
                self.sums_copied = ring("sums_copied")
                self.messages_ready = ring("messages_ready")
                self.part1_ready = ring("part1_ready")
                self.rest_ready = ring("rest_ready")
                self.part2_ready = ring("part2_ready")
                self.parts_ready = ring("parts_ready")
                self.onehot_ready = ring("onehot_ready")
                self.scattered = ring("scattered")
                self.windows_split = ring("windows_split")
                self.dve_body = sem(f"l{n}_dve_body")
                self.dve_prologue = sem(f"l{n}_dve_prologue")
                self.dve_tail = sem(f"l{n}_dve_tail")
                self.act_steps = sem(f"l{n}_act_steps")

        layers = [LayerSemaphores(0), LayerSemaphores(1)]

        block = ctx.enter_context(nc.Block())

        def passes(eng):
            eng.wait_ge(windows_known, 1)
            return eng.value_load(passes_i[0:1, 0:1], min_val=1, max_val=PASSES_ALL)

        def round_of(eng, j, i):
            return eng.snap(j * ROUNDS + (i + 1))

        def next_chunk(z, r):
            return 1 - z, r + z

        @block.sync
        def _(sp):
            sp.dma_start(dst_i[0:N_GROUPS // 4, :], dst_rows).then_inc(loaded["dst_rows"], 16)
            sp.dma_start(dst_t[:], dst).then_inc(loaded["dst"], 16)
            sp.dma_start(xs, x_self).then_inc(loaded["self"], 16)
            sp.dma_start(si_sb[:], si).then_inc(loaded["self"], 16)
            sp.dma_start(table[:, 0:BLOCKS, :], x_nodes).then_inc(loaded["nodes"], 16)
            sp.dma_start(rel_sb[:], rel[:, 0:PART_TILES, :]).then_inc(loaded["rel"], 16)
            sp.dma_start(w1_sb[:], w1_0).then_inc(loaded["weights"], 16)
            sp.dma_start(b1_sb[:, 0:1], b1_0).then_inc(loaded["weights"], 16)
            sp.dma_start(w2_sb[0][:], w2_0).then_inc(loaded["weights"], 16)
            sp.dma_start(ident[:], identity).then_inc(loaded["weights"], 16)
            sp.dma_start(w1c_sb[:], w1_1).then_inc(loaded["l1_weights"], 16)
            sp.dma_start(b1_sb[0:HID, 1:2], b1_1).then_inc(loaded["l1_weights"], 16)
            sp.dma_start(w2_sb[1][:], w2_1).then_inc(loaded["l1_weights"], 16)
            for s in layers:
                for semaphore, count in s.per_chunk:
                    sp.sem_inc(semaphore, count)
            sp.wait_ge(windows_known, 1)
            sp.dma_start(rem_dram.rearrange("(r c) -> r c", c=4), rem_f[0:N_GROUPS // 4, :]
                         ).then_inc(windows_stored, 16)
            sp.dma_start(off_dram.rearrange("(r c) -> r c", c=4), off_i[0:N_GROUPS // 4, :]
                         ).then_inc(windows_stored, 16)
            sp.wait_ge(windows_stored, 32)
            sp.dma_start(rem_sb[:], rem_dram.unsqueeze(0).broadcast_to([P, N_GROUPS])).then_inc(loaded["rem"], 16)
            sp.dma_start(offs0[:, GROUPS:], off_dram.unsqueeze(0)).then_inc(loaded["offs"], 16)
            for part in range(FRAME_PARTS):
                c0 = part * PART_TILES * GEO[1]
                if part:
                    sp.wait_ge(rel_used, part)
                    sp.dma_start(rel_sb[:], rel[:, part * PART_TILES:(part + 1) * PART_TILES, :]
                                 ).then_inc(loaded["rel"], 16)
                sp.wait_ge(frames_ready, part + 1)
                sp.dma_start(frame_dram[:, c0:c0 + PART_TILES * GEO[1]], prod[:, 0:PART_TILES * GEO[1]]
                             ).then_inc(frames_stored, 16)

            def stream(n, count):
                s = layers[n]
                with sp.Fori(0, count) as j:
                    with sp.Fori(0, ROUNDS) as i:
                        r = round_of(sp, j, i)
                        for z in range(RING):
                            k = i * RING + z
                            sp.wait_ge(s.rows_read[z], r)
                            sp.dma_start(src_sb[z][:], src[bass.ds(k, 1)].rearrange("k p t -> p (k t)")
                                         ).then_inc(s.src_loaded[z], 16)
                            if n == 0:
                                sp.wait_ge(s.hidden_summed[z], r * 2)
                                sp.dma_start(mlp_sb[z][:, 0:SET], feat[bass.ds(k, 1)].rearrange("k p c -> p (k c)")
                                             ).then_inc(s.mlp_loaded[z], 16)
                                sp.wait_ge(s.geo_used[z], r)
                                sp.dma_start(geo_sb[z][:, 0:TILES * GEO[0]],
                                             sh[bass.ds(k, 1)].rearrange("k p c -> p (k c)")
                                             ).then_inc(s.geo_loaded[z], 16)
                            else:
                                sp.wait_ge(s.hidden_ready[z], r * 2)
                                sp.dma_start(mlp_sb[z][0:HID, :],
                                             dist[bass.ds(k, 1), :].broadcast_to([HID, CHUNK])
                                             ).then_inc(s.mlp_loaded[z], 16)
                                sp.wait_ge(s.geo_used[z], r)
                                sp.dma_start(geo_sb[z][:],
                                             frame_dram[:, bass.ds(k * (TILES * GEO[1]), TILES * GEO[1])]
                                             ).then_inc(s.geo_loaded[z], 16)

            count = passes(sp)
            stream(0, count)
            sp.wait_ge(nodes_ready, 1)
            sp.dma_start(x1.rearrange("(b p) f -> p b f", p=P), table[:, 0:BLOCKS, :]).then_inc(x1_stored, 16)
            sp.wait_ge(frames_stored, 16 * FRAME_PARTS)
            stream(1, count)
            sp.wait_ge(nodes_ready, 2)
            whole = N_NODES // P
            sp.dma_start(out[0:whole * P, :].rearrange("(b p) f -> p b f", p=P), table[:, 0:whole, :]
                         ).then_inc(out_stored, 16)
            sp.dma_start(out[whole * P:, :], table[0:N_NODES - whole * P, whole, :]).then_inc(out_stored, 16)
            sp.wait_ge(out_stored, 32)

        @block.gpsimd
        def _(pool):
            nc.gpsimd.iota(iota[:], pattern=[[1, P]], base=0, channel_multiplier=0,
                           allow_small_or_imprecise_dtypes=True)
            nc.gpsimd.iota(iota_p[:], pattern=[[0, 1]], base=0, channel_multiplier=1,
                           allow_small_or_imprecise_dtypes=True).then_inc(iota_ready, 1)
            pool.wait_ge(spans_reduced, 1)
            nc.gpsimd.partition_all_reduce(span_max[:, 1:2], span_max[:, 0:1], P,
                                           bass.bass_isa.ReduceOp.max).then_inc(spans_known, 1)

            def gather(n, count):
                s = layers[n]
                table_rows = x if n == 0 else x1
                with pool.Fori(0, count) as j:
                    with pool.Fori(0, ROUNDS) as i:
                        r = round_of(pool, j, i)
                        for z in range(RING):
                            pool.wait_ge(s.rows_read[z], r)
                            pool.wait_ge(s.rows_copied[z], r)
                            pool.wait_ge(s.src_loaded[z], r * 16 + 16)
                            pool.sem_inc(gather_turns, 1)
                            for t in range(TILES):
                                nc.gpsimd.indirect_dma_start(
                                    out=rows[z][:, t, :], out_offset=None, in_=table_rows,
                                    in_offset=bass.IndirectOffsetOnAxis(ap=src_sb[z][:, t:t + 1], axis=0),
                                ).then_inc(s.rows_gathered[z], 16)

            count = passes(pool)
            gather(0, count)
            pool.wait_ge(x1_stored, 16)
            gather(1, count)

        @block.scalar
        def _(act):
            for part in range(FRAME_PARTS):
                act.wait_ge(lengths_squared, part + 1)
                length = work[:, 0:PART_TILES]
                nc.scalar.activation(length, length, ACT.Sqrt).then_inc(lengths_ready, 1)

            def hide(n, z, r, half):
                s = layers[n]
                c0 = half * 2 * SET
                if half == 0:
                    act.wait_ge(s.weights_ready[z], r * HALVES[n])
                if n == 0:
                    act.wait_ge(s.hidden_summed[z], r * 2 + half + 1)
                    nc.scalar.activation(hidden[0:HID, z, c0:c0 + SET], hps[0:HID, :], ACT.Relu,
                                         bias=b1_sb[0:HID, 0:1])
                    nc.scalar.activation(hidden[0:HID, z, c0 + SET:c0 + 2 * SET], hps[HID:P, :], ACT.Relu,
                                         bias=b1_sb[HID:P, 0:1]).then_inc(s.hidden_ready[z], 1)
                else:
                    if half == 0:
                        act.wait_ge(s.mlp_loaded[z], r * 16 + 16)
                    nc.scalar.activation(hidden[0:HID, z, c0:c0 + 2 * SET], mlp_sb[z][0:HID, c0:c0 + 2 * SET],
                                         ACT.Relu, bias=b1_sb[0:HID, 1:2], scale=w1c_sb[:, 0:1]
                                         ).then_inc(s.hidden_ready[z], 1)

            def copy_rows(n, z, r):
                s = layers[n]
                act.wait_ge(s.weights_used[z], r * HALVES[n])
                act.wait_ge(s.rows_gathered[z], r * (16 * TILES))
                s_ = rows[z][:, :, 0:MUL]
                if n == 0:
                    qa = q_sb[z][:, 0:TILES * 3 * MUL].rearrange("p (t a i) -> p t a i", t=TILES, a=3)
                    nc.scalar.activation(qa[:, :, 2, :], s_, ACT.Copy).then_inc(s.rows_copied[z], 1)
                else:
                    q = q_sb[z][:].rearrange("p (t a i) -> p t a i", t=TILES, i=MUL)
                    nc.scalar.activation(q[:, :, 0, :], s_, ACT.Copy)
                    nc.scalar.activation(q[:, :, 2, :], s_, ACT.Copy).then_inc(s.rows_copied[z], 1)

            def complete_q(z, r):
                s = layers[1]
                q = q_sb[z][:].rearrange("p (t a i) -> p t a i", t=TILES, i=MUL)
                act.wait_ge(s.rows_read[z], r + 1)
                nc.scalar.activation(q[:, :, 1, :], q[:, :, 3, :], ACT.Copy).then_inc(s.q_completed[z], 1)

            def copy_plan(n, k, z, r, steps):
                act.wait_ge(layers[n].windows_split[z], r)
                steps.done(nc.scalar.activation(plan_sb[z][:], plan[:, bass.ds(k, 1), :].rearrange("p k c -> p (k c)"),
                                                ACT.Copy))

            def distances(n, z, r, half, steps):
                s = layers[n]
                if half == 0:
                    steps.need(steps.n)
                    act.wait_ge(s.onehot_ready[1 - z], r + z)
                for t in range(half * TILES // 2, (half + 1) * TILES // 2):
                    ins = nc.scalar.activation(gap[:, t, :], iota[:], ACT.Abs, bias=plan_sb[z][:, t:t + 1])
                steps.done(ins)

            def one_hots(n, z, steps):
                s = layers[n]
                for half in range(2):
                    steps.need(steps.n - 1 + half)
                    t0, t1 = half * TILES // 2, (half + 1) * TILES // 2
                    ins = nc.scalar.activation(onehot[z][:, t0:t1, :], gap[:, t0:t1, :], ACT.Relu, scale=-1.0, bias=1.0)
                ins.then_inc(s.onehot_ready[z], 1)

            def cut_first(n, z, r):
                s = layers[n]
                act.wait_ge(s.messages_ready[z], r + 1)
                nc.scalar.activation(parts[z][:, :, 0, :], msg[:], ACT.Copy).then_inc(s.part1_ready[z], 1)

            def cut_second(n, z, r):
                s = layers[n]
                act.wait_ge(s.rest_ready[z], r + 1)
                nc.scalar.activation(parts[z][:, :, 1, :], rest[:], ACT.Copy).then_inc(s.part2_ready[z], 1)

            def copy_sums(n, z, r):
                s = layers[n]
                a, b = (t * PATHS[n] * MUL for t in PE_TILES[n])
                act.wait_ge(s.products_summed[z], r + 1)
                nc.scalar.activation(sums[:, a:b], red[:, 0:b - a], ACT.Copy).then_inc(s.sums_copied[z], 1)

            def split_windows(n, z, r):
                s = layers[n]
                act.wait_ge(s.scattered[z], r + 1)
                for g in range(GROUPS):
                    for w in range(2):
                        ins = nc.scalar.activation(split[z][:, g, w * FEAT:(w + 1) * FEAT],
                                                   acc[z][:, g * FEAT:(g + 1) * FEAT], ACT.Identity,
                                                   scale=plan_sb[z][:, TILES + g * 2 + w:TILES + g * 2 + w + 1])
                ins.then_inc(s.windows_split[z], 1)

            def loop(n, count):
                s = layers[n]

                def body(k, z, r, last, steps):
                    z1, r1 = next_chunk(z, r)
                    tail = last and z == RING - 1
                    if not tail:
                        copy_plan(n, k + 1, z1, r1, steps)
                        if n == 0:
                            copy_rows(n, z1, r1)
                        distances(n, z1, r1, 0, steps)
                    cut_first(n, z, r)
                    if not tail:
                        distances(n, z1, r1, 1, steps)
                        if n == 0:
                            one_hots(n, z1, steps)
                    cut_second(n, z, r)
                    if not last:
                        hide(n, z, r + 1, 0)
                        if n == 1:
                            hide(n, z, r + 1, 1)
                    if n == 1:
                        if not tail:
                            one_hots(n, z1, steps)
                        if not last:
                            copy_rows(n, z, r + 1)
                    if n == 0:
                        split_windows(n, z, r)
                        if not last:
                            hide(n, z, r + 1, 1)
                    if n == 1 and not last:
                        complete_q(z, r + 1)
                    if not tail:
                        copy_sums(n, z1, r1)
                    if n == 1:
                        split_windows(n, z, r)

                with act.Fori(0, count) as j:
                    act.wait_ge(windows_moved, (0 if n == 0 else count + 1) + j + 1)
                    r0 = round_of(act, j, 0)
                    steps = Steps(act, s.act_steps, (r0 - 1) * (RING * 3))
                    for z in range(RING):
                        for half in range(2):
                            hide(n, z, r0, half)
                    copy_plan(n, 0, 0, r0, steps)
                    copy_rows(n, 0, r0)
                    if n == 1:
                        complete_q(0, r0)
                    for half in range(2):
                        distances(n, 0, r0, half, steps)
                    one_hots(n, 0, steps)
                    if n == 1:
                        copy_rows(n, 1, r0)
                    copy_sums(n, 0, r0)
                    if n == 1:
                        complete_q(1, r0)
                    with act.Fori(0, ROUNDS - 1) as i:
                        r = round_of(act, j, i)
                        steps = Steps(act, s.act_steps, (r - 1) * (RING * 3) + 3)
                        for z in range(RING):
                            body(i * RING + z, z, r, False, steps)
                    r = round_of(act, j, ROUNDS - 1)
                    steps = Steps(act, s.act_steps, (r - 1) * (RING * 3) + 3)
                    for z in range(RING):
                        body((ROUNDS - 1) * RING + z, z, r, True, steps)

            def deviations(n):
                act.wait_ge(var_ready, n + 1)
                nc.scalar.activation(node_b[:], node_a[:], ACT.Sqrt, scale=1.0 / FEAT, bias=eps[:, 0:1]
                                     ).then_inc(std_ready, 1)

            act.wait_ge(loaded["weights"], 64)
            act.wait_ge(loaded["l1_weights"], 48)
            act.wait_ge(iota_ready, 1)
            act.wait_ge(consts_ready, 1)
            count = passes(act)
            loop(0, count)
            deviations(0)
            loop(1, count)
            deviations(1)

        @block.tensor
        def _(pe):
            pe.wait_ge(loaded["self"], 32)
            for r in range(-(-SELF_CHUNKS // 4)):
                if r >= 4:
                    pe.wait_ge(self_added, r - 3)
                for c in range(4 * r, min(4 * r + 4, SELF_CHUNKS)):
                    col = (r % 4) * 512 + (c % 4) * P
                    ins = nc.tensor.matmul(wps[:, col:col + P], xs[:, c, :], si_sb[:], start=True, stop=True)
                ins.then_inc(self_ready, 1)

            def sum_hidden(n, z, r, half):
                s = layers[n]
                if half == 0:
                    pe.wait_ge(s.mlp_loaded[z], r * 16 + 16)
                    pe.wait_ge(s.hidden_ready[1 - z], (r + z) * 2)
                else:
                    pe.wait_ge(s.hidden_ready[z], r * 2 + 1)
                nc.tensor.matmul(hps[:], w1_sb[:, half, :], mlp_sb[z][:, 0:SET], start=True, stop=True
                                 ).then_inc(s.hidden_summed[z], 1)

            def weigh(n, z, r, halves, first=False):
                s = layers[n]
                H, T = HALVES[n], HALF_TILES[n]
                w2 = w2_sb[n][:].rearrange("p a c -> p (a c)")
                for q in halves:
                    if q == 0 or q == H // 2:
                        pe.wait_ge(s.hidden_ready[z], r * 2 + (1 if q == 0 else 2))
                    if q >= 2:
                        pe.wait_ge(s.weights_used[z], r * H + (q - 1))
                    elif first:
                        pe.wait_ge(s.weights_used[1 - z], r * H)
                    else:
                        pe.wait_ge(s.weights_used[1 - z], (r + z) * H + (q - 1))
                    for t in range(T):
                        col = (q % 2) * 1024 + t * (1024 // T)
                        e0 = (q * T + t) * P
                        ins = nc.tensor.matmul(wps[:, col:col + W_PATHS[n] * MM], hidden[:, z, e0:e0 + P], w2,
                                               start=True, stop=True)
                    ins.then_inc(s.weights_ready[z], 1)

            def sum_products(n, z, r):
                s = layers[n]
                a, b = (t * PATHS[n] * MM for t in PE_TILES[n])
                pr = prod[:, a:b].rearrange("p (o i) -> p i o", i=MUL)
                pe.wait_ge(s.weights_used[z], r * HALVES[n] + PE_HALVES[n])
                pe.wait_ge(s.sums_copied[1 - z], r + z)
                for i in range(MUL):
                    ins = nc.tensor.matmul(red[:, 0:(b - a) // MUL], ident[:], pr[:, i, :], start=(i == 0),
                                           stop=(i == MUL - 1))
                ins.then_inc(s.products_summed[z], 1)

            def scatter(n, z, r):
                s = layers[n]
                pe.wait_ge(s.onehot_ready[z], r + 1)
                pe.wait_ge(s.parts_ready[z], r + 1)
                pe.wait_ge(s.windows_split[z], r)
                for t in range(TILES):
                    g, tg = divmod(t, GROUP_TILES)
                    for part in range(3):
                        ins = nc.tensor.matmul(acc[z][:, g * FEAT:(g + 1) * FEAT], onehot[z][:, t, :],
                                               parts[z][:, t, part, :], start=(tg == 0 and part == 0),
                                               stop=(tg == GROUP_TILES - 1 and part == 2))
                ins.then_inc(s.scattered[z], 1)

            def loop(n, count):
                H = HALVES[n]

                def body(z, r, last):
                    z1, r1 = next_chunk(z, r)
                    if last and z == RING - 1:
                        scatter(n, z, r)
                        return
                    if n == 0:
                        weigh(n, z1, r1, range(2, H))
                        if not last:
                            sum_hidden(n, z, r + 1, 0)
                        scatter(n, z, r)
                        if not last:
                            sum_hidden(n, z, r + 1, 1)
                        sum_products(n, z1, r1)
                        if not last:
                            weigh(n, z, r + 1, (0, 1))
                    else:
                        weigh(n, z1, r1, range(2, H))
                        if not last:
                            weigh(n, z, r + 1, (0,))
                        sum_products(n, z1, r1)
                        scatter(n, z, r)
                        if not last:
                            weigh(n, z, r + 1, (1,))

                with pe.Fori(0, count) as j:
                    r0 = round_of(pe, j, 0)
                    if n == 0:
                        for half in range(2):
                            sum_hidden(n, 0, r0, half)
                    weigh(n, 0, r0, (0, 1), True)
                    if n == 0:
                        for half in range(2):
                            sum_hidden(n, 1, r0, half)
                    weigh(n, 0, r0, range(2, H))
                    sum_products(n, 0, r0)
                    weigh(n, 1, r0, (0, 1))
                    with pe.Fori(0, ROUNDS - 1) as i:
                        r = round_of(pe, j, i)
                        for z in range(RING):
                            body(z, r, False)
                    r = round_of(pe, j, ROUNDS - 1)
                    for z in range(RING):
                        body(z, r, True)

            pe.wait_ge(loaded["weights"], 64)
            pe.wait_ge(consts_ready, 1)
            pe.wait_ge(w2_scaled, 1)
            count = passes(pe)
            loop(0, count)
            loop(1, count)

        @block.vector
        def _(dve):
            st = Steps(dve, setup_steps)

            def chain(instruction):
                st.need(st.done(instruction))

            ROWS = N_GROUPS // 4
            st.done(nc.vector.memset(span_max[:], -1.0))
            st.done(nc.vector.memset(lowest[:], 0.0))
            dve.wait_ge(loaded["dst_rows"], 16)
            node = work[0:ROWS, 0:4 * GROUP]
            pad = work[0:ROWS, 4 * GROUP:8 * GROUP]
            chain(nc.vector.tensor_copy(node, dst_i[0:ROWS, :]))
            st.done(nc.vector.tensor_scalar(pad, node, 0.0, FAR, ALU.is_lt, ALU.mult))
            chain(nc.vector.tensor_reduce(highest[0:ROWS, :], node.rearrange("r (g e) -> r g e", g=4), AX_X, ALU.max))
            chain(nc.vector.tensor_tensor(node, node, pad, ALU.add))
            chain(nc.vector.tensor_reduce(lowest[0:ROWS, :], node.rearrange("r (g e) -> r g e", g=4), AX_X, ALU.min))
            chain(nc.vector.tensor_tensor(span[0:ROWS, :], highest[0:ROWS, :], lowest[0:ROWS, :], ALU.subtract))
            nc.vector.tensor_reduce(span_max[0:ROWS, 0:1], span[0:ROWS, :], AX_X, ALU.max).then_inc(spans_reduced, 1)
            chain(nc.vector.tensor_scalar(lowest[:], lowest[:], float(N_NODES - 1), None, ALU.min))
            dve.wait_ge(spans_known, 1)
            chain(nc.vector.tensor_scalar(fits[:], span_max[:, 1:2], float(P) - 0.5, None, ALU.is_lt))
            chain(nc.vector.tensor_scalar(passes_f[:], fits[:], float(1 - PASSES_ALL), float(PASSES_ALL),
                                          ALU.mult, ALU.add))
            st.done(nc.vector.tensor_copy(passes_i[:], passes_f[:]))
            chain(nc.vector.tensor_scalar(lowest[:], lowest[:], fits[:, 0:1], None, ALU.mult))
            chain(nc.vector.tensor_copy(start_i[:], lowest[:]))
            st.done(nc.vector.tensor_scalar(off_i[:], start_i[:], 7, 5, ALU.arith_shift_right, ALU.logical_shift_left))
            chain(nc.vector.tensor_single_scalar(rem_i[:], start_i[:], P - 1, ALU.bitwise_and))
            chain(nc.vector.tensor_copy(rem_f[:], rem_i[:]))
            dve.nop().then_inc(windows_known, 1)

            dve.wait_ge(loaded["weights"], 64)
            chain(nc.vector.tensor_scalar(w2_sb[0][:], w2_sb[0][:], ALPHA, None, ALU.mult))
            st.done(nc.vector.tensor_scalar(w2_sb[0][:, 1, :], w2_sb[0][:, 1, :], C110, None, ALU.mult))
            dve.wait_ge(loaded["l1_weights"], 48)
            w2 = w2_sb[1]
            for path, factor in ((3, K_11_2), (0, K_00), (1, K_01), (2, K_10), (6, K_11_1)):
                st.done(nc.vector.tensor_scalar(w2[:, path, :], w2[:, path, :], factor, None, ALU.mult))
            st.need(st.n)
            chain(nc.vector.tensor_scalar(w2_tmp[:], w2[:, 3, :], -1.0 / 3.0, None, ALU.mult))
            chain(nc.vector.scalar_tensor_tensor(out=w2[:, 4, :], in0=w2[:, 4, :], scalar=K_11_0, in1=w2_tmp[:],
                                                 op0=ALU.mult, op1=ALU.add))
            st.done(nc.vector.tensor_tensor(w2[:, 3, :], w2[:, 3, :], w2[:, 4, :], ALU.add))
            chain(nc.vector.tensor_tensor(w2[:, 5, :], w2[:, 4, :], w2[:, 6, :], ALU.add))
            chain(nc.vector.tensor_tensor(w2[:, 4, :], w2[:, 4, :], w2[:, 6, :], ALU.subtract))
            dve.nop().then_inc(w2_scaled, 1)

            dve.wait_ge(loaded["nodes"], 16)
            st.done(nc.vector.memset(table[:, BLOCKS, :], 0.0))
            for r in range(-(-SELF_CHUNKS // 4)):
                dve.wait_ge(self_ready, r + 1)
                b0, b1 = 16 * r, min(16 * r + 16, BLOCKS)
                nc.vector.scalar_tensor_tensor(
                    out=table[:, b0:b1, :],
                    in0=wps[:, (r % 4) * 512:(r % 4) * 512 + (b1 - b0) * FEAT].rearrange("p (b f) -> p b f", f=FEAT),
                    scalar=SI_SCALE, in1=table[:, b0:b1, :], op0=ALU.mult, op1=ALU.add).then_inc(self_added, 1)
            dve.wait_ge(self_added, -(-SELF_CHUNKS // 4))
            chain(nc.vector.memset(hidden[HID:P, :, :], 0.0))
            st.done(nc.vector.memset(hidden[HID:HID + 1, :, :], 1.0))
            st.done(nc.vector.memset(eps[:], LN_EPS))

            dve.wait_ge(loaded["dst"], 16)
            target = work[:, 0:CHUNKS * TILES]
            rest_ = work[:, CHUNKS * TILES:2 * CHUNKS * TILES]
            chain(nc.vector.tensor_copy(target, dst_t[:]))
            chain(nc.vector.tensor_single_scalar(dst_t[:], dst_t[:], P - 1, ALU.bitwise_and))
            negkey0 = plan0[:, :, 0:TILES]

            def by_chunk(ap):
                return ap.rearrange("p (k t) -> p k t", t=TILES)

            st.done(nc.vector.tensor_scalar(negkey0, by_chunk(target), 0.0, FAR, ALU.is_lt, ALU.mult))
            chain(nc.vector.tensor_copy(rest_, dst_t[:]))
            chain(nc.vector.tensor_tensor(rest_, target, rest_, ALU.subtract))
            st.done(nc.vector.tensor_tensor(negkey0, negkey0, by_chunk(target), ALU.subtract))
            chain(nc.vector.tensor_scalar(rest_, rest_, fits[:, 0:1], None, ALU.mult))
            chain(nc.vector.tensor_tensor(negkey0, negkey0, by_chunk(rest_), ALU.add))

            st.done(nc.vector.memset(offs0[:, 0:GROUPS], 0))
            dve.wait_ge(iota_ready, 1)
            dve.wait_ge(loaded["rem"], 16)
            masks = plan0[:, :, TILES:PLAN].rearrange("p k (g w) -> p k g w", w=2)
            rem_g = rem_sb[:].rearrange("p (k g) -> p k g", g=GROUPS)
            st.done(nc.vector.tensor_scalar(masks[:, :, :, 0], rem_g, iota_p[:, 0:1], None, ALU.is_le))
            chain(nc.vector.tensor_scalar(masks[:, :, :, 1], rem_g, iota_p[:, 0:1], None, ALU.is_gt))
            dve.nop().then_inc(consts_ready, 1)

            frame = prod[:, 0:PART_TILES * GEO[1]].rearrange("p (t c) -> p t c", c=GEO[1])

            def col(c):
                return frame[:, :, c]

            u0, u1, u2, a0, a1, a2, b0_, b1_, b2_ = (col(c) for c in range(GEO[1]))
            length = work[:, 0:PART_TILES]
            h = work[:, PART_TILES:2 * PART_TILES]
            sign = work[:, 2 * PART_TILES:3 * PART_TILES]
            tmp = work[:, 3 * PART_TILES:4 * PART_TILES]
            tmp2 = work[:, 4 * PART_TILES:5 * PART_TILES]
            for part in range(FRAME_PARTS):
                dve.wait_ge(loaded["rel"], 16 * (part + 1))
                if part:
                    dve.wait_ge(frames_stored, 16 * part)
                sq = work[:, PART_TILES:4 * PART_TILES].rearrange("p (t c) -> p t c", c=3)
                chain(nc.vector.tensor_tensor(sq, rel_sb[:], rel_sb[:], ALU.mult))
                nc.vector.tensor_reduce(length, sq, AX_X, ALU.add).then_inc(lengths_squared, 1)
                dve.wait_ge(lengths_ready, part + 1)
                chain(nc.vector.reciprocal(h, length))
                st.done(nc.vector.tensor_tensor(frame[:, :, 0:2], rel_sb[:, :, 1:3],
                                                h.unsqueeze(2).broadcast_to([P, PART_TILES, 2]), ALU.mult))
                chain(nc.vector.tensor_tensor(u2, rel_sb[:, :, 0], h, ALU.mult))
                dve.nop().then_inc(rel_used, 1)
                chain(nc.vector.tensor_scalar(sign, u2, 0.0, 2.0, ALU.is_ge, ALU.mult))
                chain(nc.vector.tensor_scalar(sign, sign, -1.0, None, ALU.add))
                chain(nc.vector.tensor_tensor(h, sign, u2, ALU.add))
                st.done(nc.vector.scalar_tensor_tensor(out=a2, in0=u0, scalar=-1.0, in1=sign, op0=ALU.mult,
                                                       op1=ALU.mult))
                chain(nc.vector.reciprocal(h, h))
                st.done(nc.vector.tensor_scalar(b2_, u1, -1.0, None, ALU.mult))
                st.done(nc.vector.tensor_tensor(tmp, u0, h, ALU.mult))
                chain(nc.vector.tensor_tensor(tmp2, u1, h, ALU.mult))
                st.done(nc.vector.tensor_tensor(tmp, a2, tmp, ALU.mult))
                chain(nc.vector.scalar_tensor_tensor(out=b0_, in0=u0, scalar=-1.0, in1=tmp2, op0=ALU.mult,
                                                     op1=ALU.mult))
                st.done(nc.vector.tensor_tensor(tmp2, u1, tmp2, ALU.mult))
                st.done(nc.vector.tensor_tensor(a1, sign, b0_, ALU.mult))
                chain(nc.vector.tensor_scalar(a0, tmp, 1.0, None, ALU.add))
                chain(nc.vector.tensor_tensor(b1_, sign, tmp2, ALU.subtract))
                dve.nop().then_inc(frames_ready, 1)
            dve.wait_ge(frames_stored, 16 * FRAME_PARTS)
            dve.wait_ge(loaded["offs"], 16)

            flat = table[:].rearrange("p b f -> p (b f)")

            def vec_im(ap):
                return ap.rearrange("p t (i m) -> p t i m", m=3)

            def vec_mi(ap):
                return ap.rearrange("p t (i m) -> p t m i", m=3)

            def q_a(z):
                return q_sb[z][:, 0:TILES * 3 * MUL].rearrange("p (t a i) -> p t a i", t=TILES, a=3)

            def q_b(z):
                return q_sb[z][:, TILES * 3 * MUL:TILES * 6 * MUL].rearrange("p (t m i) -> p t m i", t=TILES, m=3)

            def q_all(z):
                return q_sb[z][:].rearrange("p (t a i) -> p t a i", t=TILES, i=MUL)

            def harmonics(z):
                return geo_sb[z][:, 0:TILES * GEO[0]].rearrange("p (t c) -> p t c", c=GEO[0])

            def frames(z):
                return geo_sb[z][:].rearrange("p (t f m) -> p t f m", t=TILES, m=3)

            def sums_of(n):
                return sums[:, 0:TILES * PATHS[n] * MUL].rearrange("p (t a o) -> p t a o", t=TILES, o=MUL)

            def multiply(n, z, r, q):
                s = layers[n]
                T = HALF_TILES[n]
                t0 = q * T
                C = PATHS[n] * MM
                w = wps[:, (q % 2) * 1024:(q % 2) * 1024 + 1024].rearrange("p (t c) -> p t c", t=T)
                pr = prod[:, t0 * C:(t0 + T) * C].rearrange("p (t c) -> p t c", t=T)
                dve.wait_ge(s.weights_ready[z], r * HALVES[n] + q + 1)
                if n == 0:
                    nc.vector.tensor_tensor(
                        pr[:, :, 3 * MM:6 * MM].rearrange("p t (m o i) -> p t m o i", m=3, o=MUL),
                        w[:, :, 3 * MM:4 * MM].rearrange("p t (o i) -> p t o i", o=MUL).unsqueeze(2)
                        .broadcast_to([P, T, 3, MUL, MUL]),
                        q_b(z)[:, t0:t0 + T].unsqueeze(3).broadcast_to([P, T, 3, MUL, MUL]), ALU.mult)
                    if q == 0:
                        dve.wait_ge(s.rows_copied[z], r + 1)
                    ins = nc.vector.tensor_tensor(
                        pr[:, :, 0:3 * MM].rearrange("p t (a o i) -> p t a o i", a=3, o=MUL),
                        w[:, :, 0:3 * MM].rearrange("p t (a o i) -> p t a o i", a=3, o=MUL),
                        q_a(z)[:, t0:t0 + T].unsqueeze(3).broadcast_to([P, T, 3, MUL, MUL]), ALU.mult)
                else:
                    if q == 0:
                        dve.wait_ge(s.q_completed[z], r + 1)
                    ins = nc.vector.tensor_tensor(
                        pr.rearrange("p t (a o i) -> p t a o i", a=7, o=MUL),
                        w[:, :, 0:C].rearrange("p t (a o i) -> p t a o i", a=7, o=MUL),
                        q_all(z)[:, t0:t0 + T].unsqueeze(3).broadcast_to([P, T, 7, MUL, MUL]), ALU.mult)
                ins.then_inc(s.weights_used[z], 1)

            def sum_tiles(n, z, r, which, st):
                s = layers[n]
                t0, t1 = DVE_SUMS[n][which]
                C = PATHS[n] * MM
                dve.wait_ge(s.weights_used[z], r * HALVES[n] + -(-t1 // HALF_TILES[n]))
                st.done(nc.vector.tensor_reduce(
                    sums[:, t0 * PATHS[n] * MUL:t1 * PATHS[n] * MUL],
                    prod[:, t0 * C:t1 * C].rearrange("p (o i) -> p o i", i=MUL), AX_X, ALU.add))

            def first_rest(n, z, r):
                s = layers[n]
                dve.wait_ge(s.part1_ready[z], r + 1)
                nc.vector.tensor_tensor(rest[:], msg[:], parts[z][:, :, 0, :], ALU.subtract).then_inc(s.rest_ready[z], 1)

            def last_part(n, z, r):
                s = layers[n]
                dve.wait_ge(s.part2_ready[z], r + 1)
                nc.vector.tensor_tensor(parts[z][:, :, 2, :], rest[:], parts[z][:, :, 1, :], ALU.subtract
                                        ).then_inc(s.parts_ready[z], 1)

            def project(n, z, r, st):
                s = layers[n]
                dve.wait_ge(s.geo_loaded[z], r * 16 + 16)
                dve.wait_ge(s.rows_gathered[z], r * (16 * TILES))
                v_ = rows[z][:, :, MUL:FEAT]
                if n == 0:
                    ins = nc.vector.tensor_tensor(
                        vec_im(t_a[:, 0:TILES * 3 * MUL].rearrange("p (t c) -> p t c", t=TILES)), vec_im(v_),
                        harmonics(z)[:, :, 1:4].unsqueeze(2).broadcast_to([P, TILES, MUL, 3]), ALU.mult)
                else:
                    ins = nc.vector.tensor_tensor(
                        t_a[:].rearrange("p (t f i m) -> p t f i m", t=TILES, f=3, m=3),
                        vec_im(v_).unsqueeze(2).broadcast_to([P, TILES, 3, MUL, 3]),
                        frames(z).unsqueeze(3).broadcast_to([P, TILES, 3, MUL, 3]), ALU.mult)
                return st.done(ins)

            def project_sum(n, z):
                s = layers[n]
                if n == 0:
                    ins = nc.vector.tensor_reduce(
                        q_a(z)[:, :, 1, :], t_a[:, 0:TILES * 3 * MUL].rearrange("p (t i m) -> p t i m", t=TILES, m=3),
                        AX_X, ALU.add)
                else:
                    ins = nc.vector.tensor_reduce(
                        q_sb[z][:].rearrange("p (t c) -> p t c", t=TILES)[:, :, 3 * MUL:6 * MUL],
                        t_a[:].rearrange("p (t c m) -> p t c m", t=TILES, m=3), AX_X, ALU.add)
                ins.then_inc(s.rows_read[z], 1)

            def scale_rows(z, st):
                sh0 = harmonics(z)[:, :, 0:1]
                st.done(nc.vector.tensor_tensor(q_a(z)[:, :, 0, :], rows[z][:, :, 0:MUL],
                                                sh0.broadcast_to([P, TILES, MUL]), ALU.mult))
                return st.done(nc.vector.tensor_tensor(q_b(z), vec_mi(rows[z][:, :, MUL:FEAT]),
                                                       sh0.unsqueeze(3).broadcast_to([P, TILES, 3, MUL]), ALU.mult))

            def differ(z, r, st):
                dve.wait_ge(layers[1].rows_read[z], r + 1)
                q = q_all(z)
                return st.done(nc.vector.tensor_tensor(q[:, :, 6, :], q[:, :, 4, :], q[:, :, 5, :], ALU.subtract))

            def add_window(g, cols, z, st):
                if g:
                    st.need(add_window.last)
                window = flat[:, bass.ds(cols[g], 2 * FEAT)]
                add_window.last = st.done(nc.vector.tensor_tensor(window, window, split[z][:, g, :], ALU.add))

            def load_columns(k):
                _, cols = nc.values_load_multi_w_load_instructions(
                    offs[0:1, bass.ds(k * GROUPS, GROUPS)], engines=(mybir.EngineType.DVE,), min_val=0,
                    max_val=(BLOCKS - 1) * FEAT)
                return cols

            def body0(k, z, r, st, tail):
                s = layers[0]
                z1, r1 = next_chunk(z, r)
                sm = sums_of(0)
                cols = load_columns(k)
                if not tail:
                    projected = project(0, z1, r1, st)
                st.need(0)
                dve.wait_ge(s.windows_split[z1], r + z)
                add_window(0, cols, z1, st)
                add_window(1, cols, z1, st)
                if not tail:
                    scaled = scale_rows(z1, st)
                add_window(2, cols, z1, st)
                if not tail:
                    st.need(projected)
                    project_sum(0, z1)
                along = t_b[:, 0:TILES * 3 * MUL].rearrange("p (t o m) -> p t o m", t=TILES, m=3)
                dve.wait_ge(s.sums_copied[z], r + 1)
                nc.vector.tensor_tensor(
                    along, sm[:, :, 2, :].unsqueeze(3).broadcast_to([P, TILES, MUL, 3]),
                    harmonics(z)[:, :, 1:4].unsqueeze(2).broadcast_to([P, TILES, MUL, 3]), ALU.mult
                ).then_inc(s.geo_used[z], 1)
                nc.vector.tensor_tensor(msg[:, :, 0:MUL], sm[:, :, 0, :], sm[:, :, 1, :], ALU.add)
                add_window(3, cols, z1, st)
                dve.wait_ge(s.geo_used[z], r + 1)
                nc.vector.tensor_tensor(
                    vec_im(msg[:, :, MUL:FEAT]), along, sm[:, :, 3:6, :].rearrange("p t m o -> p t o m"), ALU.add
                ).then_inc(s.messages_ready[z], 1)
                if not tail:
                    st.need(scaled)
                    dve.wait_ge(s.rows_read[z1], r1 + 1)
                    multiply(0, z1, r1, 0)
                    multiply(0, z1, r1, 1)
                first_rest(0, z, r)
                if not tail:
                    multiply(0, z1, r1, 2)
                last_part(0, z, r)
                if not tail:
                    multiply(0, z1, r1, 3)
                    for which in range(len(DVE_SUMS[0])):
                        sum_tiles(0, z1, r1, which, st)

            def prologue0(r, st):
                projected = project(0, 0, r, st)
                scaled = scale_rows(0, st)
                st.need(projected)
                project_sum(0, 0)
                st.need(scaled)
                dve.wait_ge(layers[0].rows_read[0], r + 1)
                for q in range(HALVES[0]):
                    multiply(0, 0, r, q)
                for which in range(len(DVE_SUMS[0])):
                    sum_tiles(0, 0, r, which, st)

            def body1(k, z, r, st, last, tail):
                s = layers[1]
                z1, r1 = next_chunk(z, r)
                sm = sums_of(1)
                if not tail:
                    st.need(0)
                    multiply(1, z1, r1, 0)
                else:
                    st.need(0)
                dve.wait_ge(s.sums_copied[z], r + 1)
                pair = sm[:, :, 0:4, :].rearrange("p t (b a) o -> p t b a o", a=2)
                st.done(nc.vector.tensor_tensor(
                    msg[:, :, 0:2 * MUL].rearrange("p t (b o) -> p t b o", b=2), pair[:, :, :, 0, :],
                    pair[:, :, :, 1, :], ALU.add))
                framed = st.done(nc.vector.tensor_tensor(
                    msg[:, :, 2 * MUL:FEAT].rearrange("p t (b o) -> p t b o", b=2), sm[:, :, 4:6, :],
                    sm[:, :, 6:7, :].broadcast_to([P, TILES, 2, MUL]), ALU.add))
                if not tail:
                    multiply(1, z1, r1, 1)
                st.need(framed)
                turned = t_b[:].rearrange("p (t f c) -> p t f c", t=TILES, f=3)
                nc.vector.tensor_tensor(
                    turned.rearrange("p t f (o m) -> p t f o m", m=3),
                    msg[:, :, MUL:FEAT].rearrange("p t (f o) -> p t f o", f=3).unsqueeze(4)
                    .broadcast_to([P, TILES, 3, MUL, 3]),
                    frames(z).unsqueeze(3).broadcast_to([P, TILES, 3, MUL, 3]), ALU.mult).then_inc(s.geo_used[z], 1)
                if not tail:
                    multiply(1, z1, r1, 2)
                dve.wait_ge(s.geo_used[z], r + 1)
                nc.vector.tensor_reduce(msg[:, :, MUL:FEAT], turned.rearrange("p t f c -> p t c f"), AX_X, ALU.add
                                        ).then_inc(s.messages_ready[z], 1)
                if not tail:
                    multiply(1, z1, r1, 3)
                    multiply(1, z1, r1, 4)
                first_rest(1, z, r)
                if not tail:
                    multiply(1, z1, r1, 5)
                last_part(1, z, r)
                if not tail:
                    multiply(1, z1, r1, 6)
                if not last:
                    projected = project(1, z, r + 1, st)
                if not tail:
                    multiply(1, z1, r1, 7)
                if not last:
                    st.need(projected)
                    project_sum(1, z)
                if not tail:
                    sum_tiles(1, z1, r1, 0, st)
                cols = load_columns(k)
                dve.wait_ge(s.windows_split[z1], r + z)
                add_window(0, cols, z1, st)
                if not last:
                    differ(z, r + 1, st)
                add_window(1, cols, z1, st)
                if not tail:
                    sum_tiles(1, z1, r1, 1, st)
                add_window(2, cols, z1, st)
                add_window(3, cols, z1, st)

            def prologue1(r, st):
                for z in range(RING):
                    st.need(project(1, z, r, st))
                    project_sum(1, z)
                    st.need(differ(z, r, st))
                for q in range(HALVES[1]):
                    multiply(1, 0, r, q)
                for which in range(len(DVE_SUMS[1])):
                    sum_tiles(1, 0, r, which, st)

            def body(n, k, z, r, st, last, tail):
                if n == 0:
                    body0(k, z, r, st, tail)
                else:
                    body1(k, z, r, st, last, tail)

            def loop(n, count):
                s = layers[n]
                with dve.Fori(0, count) as j:
                    r0 = round_of(dve, j, 0)
                    st = Steps(dve, s.dve_prologue, j * PROLOGUE_STEPS[n])
                    st.need(st.done(nc.vector.memset(split[1][:], 0.0)))
                    (prologue0, prologue1)[n](r0, st)
                    assert st.n == PROLOGUE_STEPS[n], ("prologue", n, st.n)
                    st.need(st.n)
                    dve.sem_inc(dve_turns, 1)
                    bodies = CHUNKS - 1
                    with dve.Fori(0, ROUNDS - 1) as i:
                        r = round_of(dve, j, i)
                        for z in range(RING):
                            st = Steps(dve, s.dve_body, j * (bodies * BODY_STEPS[n])
                                       + i * (RING * BODY_STEPS[n]) + (z * BODY_STEPS[n] + 1))
                            body(n, i * RING + z, z, r, st, False, False)
                            assert st.n == BODY_STEPS[n], ("body", n, st.n)
                    r = round_of(dve, j, ROUNDS - 1)
                    st = Steps(dve, s.dve_body, j * (bodies * BODY_STEPS[n]) + ((bodies - 1) * BODY_STEPS[n] + 1))
                    body(n, CHUNKS - 2, 0, r, st, True, False)
                    for _ in range(st.n, BODY_STEPS[n]):
                        st.done(dve.nop())
                    st.need(st.n)
                    dve.sem_inc(dve_turns, 1)
                    st = Steps(dve, s.dve_tail, j * TAIL_STEPS[n])
                    body(n, CHUNKS - 1, 1, r, st, True, True)
                    cols = load_columns(CHUNKS)
                    dve.wait_ge(s.windows_split[1], r + 1)
                    st.need(st.n)
                    for g in range(GROUPS):
                        add_window(g, cols, 1, st)
                    st.need(st.n)
                    dve.wait_ge(s.onehot_ready[1], r + 1)
                    st.done(nc.vector.tensor_scalar(offs[:], offs[:], FEAT, None, ALU.add))
                    st.done(nc.vector.tensor_scalar(plan[:, :, 0:TILES], plan[:, :, 0:TILES], float(P), None, ALU.add))
                    assert st.n == TAIL_STEPS[n], ("tail", n, st.n)
                    st.need(st.n)
                    dve.nop().then_inc(windows_moved, 1)

            def first_windows():
                st.done(nc.vector.tensor_copy(offs[:], offs0[:]))
                chain(nc.vector.tensor_copy(plan[:], plan0[:]))
                dve.nop().then_inc(windows_moved, 1)

            def normalize(n):
                nodes = table[:, 0:BLOCKS, :]
                sq_ = work[:, 0:BLOCKS * FEAT].rearrange("p (b f) -> p b f", f=FEAT)
                chain(nc.vector.tensor_reduce(node_a[:], nodes, AX_X, ALU.add))
                chain(nc.vector.tensor_scalar(node_c[:], node_a[:], 1.0 / FEAT, None, ALU.mult))
                chain(nc.vector.tensor_tensor(nodes, nodes, node_c[:].unsqueeze(2).broadcast_to([P, BLOCKS, FEAT]),
                                              ALU.subtract))
                chain(nc.vector.tensor_tensor(sq_, nodes, nodes, ALU.mult))
                nc.vector.tensor_reduce(node_a[:], sq_, AX_X, ALU.add).then_inc(var_ready, 1)
                dve.wait_ge(std_ready, n + 1)
                chain(nc.vector.reciprocal(node_c[:], node_b[:]))
                nc.vector.tensor_tensor(nodes, nodes, node_c[:].unsqueeze(2).broadcast_to([P, BLOCKS, FEAT]),
                                        ALU.mult).then_inc(nodes_ready, 1)

            for s in layers:
                dve.sem_inc(s.dve_body, 1)
            first_windows()
            count = passes(dve)
            loop(0, count)
            normalize(0)
            first_windows()
            dve.wait_ge(x1_stored, 16)
            loop(1, count)
            normalize(1)


_OUT = ((N_NODES, FEAT), "float32")


def kernel(x, src, dst, edge_attr_3, edge_attr_32, edge_attr_4, edge_weight, L0_gnn_W1, L0_gnn_b1, L0_gnn_W2,
           L0_gnn_b2, L0_gnn_si_w0, L0_gnn_si_w1, L1_gnn_w1, L1_gnn_b1, L1_gnn_w2, L1_gnn_b2):
    import concourse.bacc as bacc
    from concourse.bass_utils import run_bass_kernel_spmd

    def padded(a, n, value):
        a = np.asarray(a)
        return np.concatenate([a, np.full((n - a.shape[0], *a.shape[1:]), value, a.dtype)])

    def by_partition(a):
        return np.swapaxes(a.reshape(CHUNKS, TILES, P, *a.shape[1:]), 1, 2)

    def all_by_partition(a):
        return np.swapaxes(by_partition(a), 0, 1).reshape(P, CHUNKS * TILES, *a.shape[1:])

    x = np.asarray(x)
    x_pad = padded(x, SELF_CHUNKS * 4 * P, 0)
    dst_p = padded(dst, EDGES, -1)
    feat = padded(edge_attr_32, EDGES, 0).reshape(CHUNKS, SETS, SET, FEAT)
    W1 = np.zeros((SETS, FEAT, 2, 2, HID), np.float32)
    for s in range(SETS):
        W1[s, :, s // 2, s % 2, :] = np.asarray(L0_gnn_W1)
    b1_0 = np.asarray(L0_gnn_b1).reshape(HID, 1)
    S = np.zeros((4, FEAT, 4, FEAT), np.float32)
    for b in range(4):
        S[b, :MUL, b, :MUL] = np.asarray(L0_gnn_si_w0)
        for m in range(3):
            S[b, MUL + m::3, b, MUL + m::3] = np.asarray(L0_gnn_si_w1)

    def with_bias(w, b, paths):
        cols = np.concatenate([c.ravel() for c in paths])
        out = np.zeros((P, len(cols)), np.float32)
        out[:HID] = np.asarray(w)[:, cols]
        out[HID] = np.asarray(b)[cols]
        return out.reshape(P, len(paths), MM)

    i, o = np.arange(MUL)[None, :], np.arange(MUL)[:, None]
    w000, w011, w101, w110 = (p * MM + i * MUL + o for p in range(4))
    uv = o * MUL + i
    R00, R01, R10 = uv, MM + uv, 2 * MM + uv
    R0, R1, R2 = (3 * MM + uv * 3 + l for l in range(3))

    arrays = {
        "x": x,
        "x_nodes": np.swapaxes(x_pad[:BLOCKS * P].reshape(BLOCKS, P, FEAT), 0, 1),
        "x_self": x_pad.reshape(SELF_CHUNKS, 4, P, FEAT).transpose(1, 3, 0, 2).reshape(P, SELF_CHUNKS, P),
        "src": by_partition(padded(src, EDGES, 0)),
        "dst": all_by_partition(dst_p),
        "dst_rows": dst_p.reshape(N_GROUPS // 4, 4 * GROUP),
        "sh": by_partition(padded(edge_attr_4, EDGES, 0)).reshape(CHUNKS, P, TILES * GEO[0]),
        "feat": np.swapaxes(feat, 2, 3).reshape(CHUNKS, P, SET),
        "rel": all_by_partition(padded(edge_attr_3, EDGES, 1)),
        "dist": padded(edge_weight, EDGES, 0).reshape(CHUNKS, CHUNK),
        "identity": np.eye(P, dtype=np.float32),
        "w1_0": W1.reshape(P, 2, 2 * HID),
        "b1_0": np.concatenate([b1_0, b1_0]),
        "w2_0": with_bias(L0_gnn_W2, L0_gnn_b2, (w000, w110, w011, w101)),
        "si": S.reshape(P, P),
        "w1_1": np.asarray(L1_gnn_w1).reshape(HID, 1),
        "b1_1": np.asarray(L1_gnn_b1).reshape(HID, 1),
        "w2_1": with_bias(L1_gnn_w2, L1_gnn_b2, (R00, R01, R10, R2, R0, R0, R1)),
    }
    nc = bacc.Bacc("TRN2", target_bir_lowering=False, num_devices=1)
    args, ins = {}, {}
    for name, a in arrays.items():
        ins[f"in_{name}"] = np.ascontiguousarray(a)
        args[name] = nc.dram_tensor(f"in_{name}", a.shape, mybir.dt.from_np(a.dtype), kind="ExternalInput").ap()
    out = nc.dram_tensor("out_0", _OUT[0], F32, kind="ExternalOutput").ap()
    build(nc, out=out, **args)
    r = run_bass_kernel_spmd(nc, [ins], core_ids=[0])
    return r.results[0]["out_0"]
```

```python
from contextlib import ExitStack
from math import pi, sqrt

import numpy as np

import concourse.bass as bass
from concourse import mybir

F32, BF16, I32 = mybir.dt.float32, mybir.dt.bfloat16, mybir.dt.int32
ALU = mybir.AluOpType
ACT = mybir.ActivationFunctionType
AX_X = mybir.AxisListType.X

P = 128
N_NODES, N_EDGES = 12500, 200000
MUL, FEAT = 8, 32
HID = 64
TILES = 16
CHUNK = TILES * P
RING = 2
CHUNKS = -(-N_EDGES // (CHUNK * RING)) * RING
ROUNDS = CHUNKS // RING
EDGES = CHUNKS * CHUNK
SETS = 4
SET = CHUNK // SETS
GROUP_TILES = 4
GROUPS = TILES // GROUP_TILES
N_GROUPS = CHUNKS * GROUPS
GROUP = GROUP_TILES * P
BLOCKS = -(-N_NODES // P)
PASSES_ALL = BLOCKS
FAR = float(4 * BLOCKS * P)
SELF_CHUNKS = -(-BLOCKS // 4)
LN_EPS = 1e-5

MM = MUL * MUL
W_PATHS, PATHS = (4, 7), (6, 7)
HALF_TILES = (4, 2)
HALVES = tuple(TILES // h for h in HALF_TILES)
PLAN = TILES + 2 * GROUPS
PE_TILES = ((0, 6), (0, 7))
PE_HALVES = tuple(-(-PE_TILES[n][1] // HALF_TILES[n]) for n in range(2))
DVE_SUMS = (((6, 11), (11, 16)), ((7, 12), (12, 16)))
GEO = (4, 9)
FRAME_PARTS = 4
PART_TILES = CHUNKS * TILES // FRAME_PARTS
ALPHA, C110, SI_SCALE = 0.25, 1.0 / sqrt(3.0), 1.0 / sqrt(MUL)
NORM0 = sqrt(4 * pi) / sqrt(2 * MUL)
NORM1 = sqrt(4 * pi) * sqrt(3.0) / sqrt(4 * MUL)
Y0, Y1 = 0.5 / sqrt(pi), sqrt(3.0 / (4 * pi))
K_00 = NORM0 * Y0
K_01 = NORM0 * Y1 / sqrt(3.0)
K_10 = NORM1 * Y1 / sqrt(3.0)
K_11_0 = NORM1 * Y0 / sqrt(3.0)
K_11_1 = NORM1 * Y1 / sqrt(6.0)
K_11_2 = NORM1 * sqrt(3.0 / (8 * pi))


class Steps:

    def __init__(self, eng, sem, base=0):
        self.eng, self.sem, self.base, self.n = eng, sem, base, 0

    def done(self, instruction):
        instruction.then_inc(self.sem, 1)
        self.n += 1
        return self.n

    def need(self, n):
        self.eng.wait_ge(self.sem, self.base + n)


BODY_STEPS, PROLOGUE_STEPS, TAIL_STEPS = (9, 10), (6, 7), (10, 12)


def build(nc, x, x_nodes, x_self, src, dst, dst_rows, sh, feat, rel, dist, identity, w1_0, b1_0, w2_0, si, w1_1, b1_1,
          w2_1, out):
    x1 = nc.dram_tensor("x1_rows", [BLOCKS * P, FEAT], F32).ap()
    frame_dram = nc.dram_tensor("frames", [P, CHUNKS * TILES * GEO[1]], F32).ap()
    off_dram = nc.dram_tensor("window_offsets", [N_GROUPS], I32).ap()
    rem_dram = nc.dram_tensor("window_remainders", [N_GROUPS], F32).ap()

    with ExitStack() as ctx:
        def sb(name, shape, dt=F32):
            return ctx.enter_context(nc.sbuf_tensor(name, shape, dt))

        def psum(name, shape, dt=F32):
            return ctx.enter_context(nc.psum_tensor(name, shape, dt))

        def sem(name):
            return ctx.enter_context(nc.semaphore(name))

        def slots(make):
            return [make(z) for z in range(RING)]

        table = sb("table", [P, BLOCKS + 1, FEAT])
        plan0 = sb("plan0", [P, CHUNKS, PLAN])
        plan = sb("plan", [P, CHUNKS, PLAN])
        offs0 = sb("offs0", [1, GROUPS + N_GROUPS], I32)
        offs = sb("offs", [1, GROUPS + N_GROUPS], I32)
        w1_sb = sb("w1_sb", [P, 2, P])
        b1_sb = sb("b1_sb", [P, 2])
        w1c_sb = sb("w1c_sb", [HID, 1])
        w2_sb = [sb(f"w2_sb{n}", [P, W_PATHS[n], MM]) for n in range(2)]
        ident = sb("ident", [P, P])
        iota = sb("iota", [P, P])
        iota_p = sb("iota_p", [P, 1])
        eps = sb("eps", [P, 1])
        node_a = sb("node_a", [P, BLOCKS])
        node_b = sb("node_b", [P, BLOCKS])
        node_c = sb("node_c", [P, BLOCKS])
        work = sb("work", [P, 8 * GROUP])
        rel_sb = sb("rel_sb", [P, CHUNKS * TILES, 3])
        dst_i = sb("dst_i", [P, 4 * GROUP], I32)
        dst_t = sb("dst_t", [P, CHUNKS * TILES], I32)
        rem_sb = sb("rem_sb", [P, N_GROUPS])
        si_sb = sb("si_sb", [P, P])
        w2_tmp = sb("w2_tmp", [P, MM])
        lowest = sb("lowest", [P, 4])
        highest = sb("highest", [P, 4])
        span = sb("span", [P, 4])
        span_max = sb("span_max", [P, 2])
        fits = sb("fits", [P, 1])
        passes_f = sb("passes_f", [P, 1])
        passes_i = sb("passes_i", [P, 1], I32)
        start_i = sb("start_i", [P, 4], I32)
        off_i = sb("off_i", [P, 4], I32)
        rem_i = sb("rem_i", [P, 4], I32)
        rem_f = sb("rem_f", [P, 4])
        src_sb = slots(lambda z: sb(f"src{z}", [P, TILES], I32))
        geo_sb = slots(lambda z: sb(f"geo{z}", [P, TILES * max(GEO)]))
        mlp_sb = slots(lambda z: sb(f"mlp{z}", [P, CHUNK]))
        rows = slots(lambda z: sb(f"rows{z}", [P, TILES, FEAT]))
        hidden = sb("hidden", [P, RING, CHUNK])
        plan_sb = slots(lambda z: sb(f"slot_plan{z}", [P, PLAN]))
        gap = sb("gap", [P, TILES, P], BF16)
        onehot = slots(lambda z: sb(f"onehot{z}", [P, TILES, P], BF16))
        parts = slots(lambda z: sb(f"parts{z}", [P, TILES, 3, FEAT], BF16))
        q_sb = slots(lambda z: sb(f"q{z}", [P, TILES * PATHS[1] * MUL]))
        split = slots(lambda z: sb(f"split{z}", [P, GROUPS, 2 * FEAT]))
        msg = sb("msg", [P, TILES, FEAT])
        rest = sb("rest", [P, TILES, FEAT])
        prod = sb("prod", [P, TILES * PATHS[1] * MM])
        sums = sb("sums", [P, TILES * PATHS[1] * MUL])
        t_a = sb("t_a", [P, TILES * 9 * MUL])
        t_b = sb("t_b", [P, TILES * 9 * MUL])
        xs = prod[:, 0:SELF_CHUNKS * P].rearrange("p (s c) -> p s c", c=P)

        wps = psum("wps", [P, 4 * 512])
        hps = psum("hps", [P, SET])
        acc = slots(lambda z: psum(f"acc{z}", [P, 512]))
        red = psum("red", [P, 512])

        loaded = {n: sem(f"{n}_loaded") for n in
                  ("dst_rows", "dst", "rel", "nodes", "self", "weights", "l1_weights", "rem", "offs")}
        windows_stored = sem("windows_stored")
        frames_stored = [sem(f"frames_stored{b}") for b in range(2)]
        windows_known = sem("windows_known")
        spans_reduced = sem("spans_reduced")
        spans_known = sem("spans_known")
        consts_ready = sem("consts_ready")
        iota_ready = sem("iota_ready")
        hidden_filled = sem("hidden_filled")
        self_ready = sem("self_ready")
        self_added = sem("self_added")
        lengths_squared = sem("lengths_squared")
        lengths_ready = sem("lengths_ready")
        frames_ready = sem("frames_ready")
        w2_scaled = sem("w2_scaled")
        var_ready = sem("var_ready")
        std_ready = sem("std_ready")
        nodes_ready = sem("nodes_ready")
        x1_stored = sem("x1_stored")
        out_stored = sem("out_stored")
        setup_steps = sem("setup_steps")
        gather_turns = sem("gather_turns")
        dve_turns = sem("dve_turns")
        windows_moved = sem("windows_moved")

        class LayerSemaphores:

            def __init__(self, n):
                self.per_chunk = []

                def ring(name, count=1):
                    made = slots(lambda z: sem(f"l{n}_{name}{z}"))
                    self.per_chunk += [(semaphore, count) for semaphore in made]
                    return made

                self.src_loaded = ring("src_loaded", 16)
                self.geo_loaded = ring("geo_loaded", 16)
                self.mlp_loaded = ring("mlp_loaded", 16)
                self.rows_gathered = slots(lambda z: sem(f"l{n}_rows_gathered{z}"))
                self.counts_reset = sem(f"l{n}_counts_reset")
                self.rows_read = ring("rows_read")
                self.rows_copied = ring("rows_copied")
                self.q_completed = ring("q_completed")
                self.geo_used = ring("geo_used")
                self.hidden_summed = ring("hidden_summed", 2)
                self.hidden_ready = ring("hidden_ready", 2)
                self.weights_ready = ring("weights_ready", HALVES[n])
                self.weights_used = ring("weights_used", HALVES[n])
                self.products_summed = ring("products_summed")
                self.sums_copied = ring("sums_copied")
                self.messages_ready = ring("messages_ready")
                self.part1_ready = ring("part1_ready")
                self.rest_ready = ring("rest_ready")
                self.part2_ready = ring("part2_ready")
                self.parts_ready = ring("parts_ready")
                self.onehot_ready = ring("onehot_ready")
                self.scattered = ring("scattered")
                self.windows_split = ring("windows_split")
                self.dve_body = sem(f"l{n}_dve_body")
                self.dve_prologue = sem(f"l{n}_dve_prologue")
                self.dve_tail = sem(f"l{n}_dve_tail")
                self.act_steps = sem(f"l{n}_act_steps")

        layers = [LayerSemaphores(0), LayerSemaphores(1)]

        block = ctx.enter_context(nc.Block())

        def passes(eng):
            eng.wait_ge(windows_known, 1)
            return eng.value_load(passes_i[0:1, 0:1], min_val=1, max_val=PASSES_ALL)

        def round_of(eng, j, i):
            return eng.snap(j * ROUNDS + (i + 1))

        def next_chunk(z, r):
            return 1 - z, r + z

        @block.sync
        def _(sp):
            sp.dma_start(dst_i[0:N_GROUPS // 4, :], dst_rows).then_inc(loaded["dst_rows"], 16)
            sp.dma_start(w1_sb[:], w1_0).then_inc(loaded["weights"], 16)
            sp.dma_start(b1_sb[:, 0:1], b1_0).then_inc(loaded["weights"], 16)
            sp.dma_start(w2_sb[0][:], w2_0).then_inc(loaded["weights"], 16)
            sp.dma_start(ident[:], identity).then_inc(loaded["weights"], 16)
            sp.dma_start(w1c_sb[:], w1_1).then_inc(loaded["l1_weights"], 16)
            sp.dma_start(b1_sb[0:HID, 1:2], b1_1).then_inc(loaded["l1_weights"], 16)
            sp.dma_start(w2_sb[1][:], w2_1).then_inc(loaded["l1_weights"], 16)
            sp.dma_start(xs, x_self).then_inc(loaded["self"], 16)
            sp.dma_start(si_sb[:], si).then_inc(loaded["self"], 16)
            sp.dma_start(table[:, 0:BLOCKS, :], x_nodes).then_inc(loaded["nodes"], 16)
            sp.dma_start(dst_t[:], dst).then_inc(loaded["dst"], 16)
            for s in layers:
                for semaphore, count in s.per_chunk:
                    sp.sem_inc(semaphore, count)
            sp.dma_start(rel_sb[:], rel).then_inc(loaded["rel"], 16)

            def stream(n, count):
                s = layers[n]
                with sp.Fori(0, count) as j:
                    with sp.Fori(0, ROUNDS) as i:
                        r = round_of(sp, j, i)
                        for z in range(RING):
                            sp.wait_ge(s.rows_read[z], r)
                            sp.dma_start(src_sb[z][:], src[bass.ds(i * RING + z, 1)].rearrange("k p t -> p (k t)")
                                         ).then_inc(s.src_loaded[z], 16)
                        for z in range(RING):
                            k = i * RING + z
                            if n == 0:
                                sp.wait_ge(s.hidden_summed[z], r * 2)
                                sp.dma_start(mlp_sb[z][:, 0:SET], feat[bass.ds(k, 1)].rearrange("k p c -> p (k c)")
                                             ).then_inc(s.mlp_loaded[z], 16)
                            else:
                                sp.wait_ge(s.hidden_ready[z], r * 2)
                                sp.dma_start(mlp_sb[z][0:HID, :],
                                             dist[bass.ds(k, 1), :].broadcast_to([HID, CHUNK])
                                             ).then_inc(s.mlp_loaded[z], 16)

            count = passes(sp)
            stream(0, count)
            sp.wait_ge(nodes_ready, 1)
            sp.dma_start(x1.rearrange("(b p) f -> p b f", p=P), table[:, 0:BLOCKS, :]).then_inc(x1_stored, 16)
            stream(1, count)
            sp.wait_ge(nodes_ready, 2)
            whole = N_NODES // P
            sp.dma_start(out[0:whole * P, :].rearrange("(b p) f -> p b f", p=P), table[:, 0:whole, :]
                         ).then_inc(out_stored, 16)
            sp.dma_start(out[whole * P:, :], table[0:N_NODES - whole * P, whole, :]).then_inc(out_stored, 16)
            sp.wait_ge(out_stored, 32)

        @block.gpsimd
        def _(pool):
            nc.gpsimd.iota(iota[:], pattern=[[1, P]], base=0, channel_multiplier=0,
                           allow_small_or_imprecise_dtypes=True)
            nc.gpsimd.iota(iota_p[:], pattern=[[0, 1]], base=0, channel_multiplier=1,
                           allow_small_or_imprecise_dtypes=True).then_inc(iota_ready, 1)
            pool.wait_ge(iota_ready, 1)
            nc.gpsimd.memset(hidden[HID:P, :, :], 0.0).then_inc(hidden_filled, 1)
            pool.wait_ge(hidden_filled, 1)
            nc.gpsimd.memset(hidden[HID:HID + 1, :, :], 1.0).then_inc(hidden_filled, 1)
            pool.wait_ge(hidden_filled, 2)
            pool.wait_ge(spans_reduced, 1)
            nc.gpsimd.partition_all_reduce(span_max[:, 1:2], span_max[:, 0:1], P,
                                           bass.bass_isa.ReduceOp.max).then_inc(spans_known, 1)

            def gather(n, z, r):
                s = layers[n]
                pool.wait_ge(s.rows_read[z], r)
                pool.wait_ge(s.rows_copied[z], r)
                pool.wait_ge(s.src_loaded[z], r * 16 + 16)
                pool.sem_inc(gather_turns, 1)
                gather_tiles(n, z, range(TILES - 1))

            def gather_tiles(n, z, tiles):
                s = layers[n]
                table_rows = x if n == 0 else x1
                for t in tiles:
                    nc.gpsimd.indirect_dma_start(
                        out=rows[z][:, t, :], out_offset=None, in_=table_rows,
                        in_offset=bass.IndirectOffsetOnAxis(ap=src_sb[z][:, t:t + 1], axis=0),
                    ).then_inc(s.rows_gathered[z], 16)

            def reset_counts(n, r):
                s = layers[n]
                for z in range(RING):
                    pool.wait_ge(s.rows_read[z], r + 1)
                    pool.wait_ge(s.rows_copied[z], r + 1)
                pool.sem_inc(gather_turns, 1)
                pool.inc_swdge_sem(s.rows_gathered, [ROUNDS * 16 * TILES] * RING, mode="sub")
                pool.sem_inc(s.counts_reset, 1)

            def gather0(count):
                with pool.Fori(0, count) as j:
                    with pool.Fori(0, ROUNDS) as i:
                        r = round_of(pool, j, i)
                        for z in range(RING):
                            gather(0, z, r)
                            gather_tiles(0, z, range(TILES - 1, TILES))
                    reset_counts(0, round_of(pool, j, ROUNDS - 1))

            def cut(z, r, gather_slot=None):
                s = layers[1]
                pool.wait_ge(s.part1_ready[z], r + 1)
                pool.sem_inc(gather_turns, 1)
                nc.gpsimd.tensor_tensor(rest[:], msg[:], parts[z][:, :, 0, :], ALU.subtract).then_inc(s.rest_ready[z], 1)
                if gather_slot is not None:
                    gather_tiles(1, gather_slot, range(TILES - 1, TILES))
                pool.wait_ge(s.part2_ready[z], r + 1)
                pool.sem_inc(gather_turns, 1)
                nc.gpsimd.tensor_tensor(parts[z][:, :, 2, :], rest[:], parts[z][:, :, 1, :], ALU.subtract
                                        ).then_inc(s.parts_ready[z], 1)

            def gather1(count):
                with pool.Fori(0, count) as j:
                    for i in range(2):
                        r = round_of(pool, j, i)
                        for z in range(RING):
                            gather(1, z, r)
                            if i * RING + z >= 3:
                                cut(1 - z, r - 2 + z, z)
                            else:
                                gather_tiles(1, z, range(TILES - 1, TILES))
                    if ROUNDS > 2:
                        with pool.Fori(0, ROUNDS - 2) as i:
                            r = round_of(pool, j, i + 2)
                            for z in range(RING):
                                gather(1, z, r)
                                cut(1 - z, r - 2 + z, z)
                    r = round_of(pool, j, ROUNDS - 1)
                    cut(1, r - 1)
                    cut(0, r)
                    cut(1, r)
                    reset_counts(1, r)

            for s in layers:
                pool.sem_inc(s.counts_reset, 1)
            count = passes(pool)
            gather0(count)
            pool.wait_ge(x1_stored, 16)
            gather1(count)

        @block.scalar
        def _(act):
            def spread_windows():
                act.wait_ge(windows_known, 1)
                act.dma_start(rem_dram.rearrange("(r c) -> r c", c=4), rem_f[0:N_GROUPS // 4, :]
                             ).then_inc(windows_stored, 16)
                act.dma_start(off_dram.rearrange("(r c) -> r c", c=4), off_i[0:N_GROUPS // 4, :]
                             ).then_inc(windows_stored, 16)
                act.wait_ge(windows_stored, 32)
                act.dma_start(rem_sb[:], rem_dram.unsqueeze(0).broadcast_to([P, N_GROUPS])).then_inc(loaded["rem"], 16)
                act.dma_start(offs0[:, GROUPS:], off_dram.unsqueeze(0)).then_inc(loaded["offs"], 16)

            def store_frames():
                act.wait_ge(lengths_squared, 1)
                lengths = work[:, 0:CHUNKS * TILES]
                nc.scalar.activation(lengths, lengths, ACT.Sqrt).then_inc(lengths_ready, 1)
                for part in range(FRAME_PARTS):
                    cols = PART_TILES * GEO[1]
                    act.wait_ge(frames_ready, part + 1)
                    act.dma_start(frame_dram[:, part * cols:(part + 1) * cols],
                                  prod[:, part % 2 * cols:part % 2 * cols + cols]).then_inc(frames_stored[part % 2], 16)

            def hide(n, z, r, half):
                s = layers[n]
                c0 = half * 2 * SET
                if half == 0:
                    act.wait_ge(s.weights_ready[z], r * HALVES[n])
                if n == 0:
                    act.wait_ge(s.hidden_summed[z], r * 2 + half + 1)
                    nc.scalar.activation(hidden[0:HID, z, c0:c0 + SET], hps[0:HID, :], ACT.Relu,
                                         bias=b1_sb[0:HID, 0:1])
                    nc.scalar.activation(hidden[0:HID, z, c0 + SET:c0 + 2 * SET], hps[HID:P, :], ACT.Relu,
                                         bias=b1_sb[HID:P, 0:1]).then_inc(s.hidden_ready[z], 1)
                else:
                    if half == 0:
                        act.wait_ge(s.mlp_loaded[z], r * 16 + 16)
                    nc.scalar.activation(hidden[0:HID, z, c0:c0 + 2 * SET], mlp_sb[z][0:HID, c0:c0 + 2 * SET],
                                         ACT.Relu, bias=b1_sb[0:HID, 1:2], scale=w1c_sb[:, 0:1]
                                         ).then_inc(s.hidden_ready[z], 1)

            def load_geo(n, k, z, r):
                s = layers[n]
                act.wait_ge(s.geo_used[z], r)
                if n == 0:
                    act.dma_start(geo_sb[z][:, 0:TILES * GEO[0]], sh[bass.ds(k, 1)].rearrange("k p c -> p (k c)")
                                  ).then_inc(s.geo_loaded[z], 16)
                else:
                    act.dma_start(geo_sb[z][:], frame_dram[:, bass.ds(k * (TILES * GEO[1]), TILES * GEO[1])]
                                  ).then_inc(s.geo_loaded[z], 16)

            def copy_rows(n, i, z, r):
                s = layers[n]
                act.wait_ge(s.weights_used[z], r * HALVES[n])
                act.wait_ge(s.rows_gathered[z], i * (16 * TILES) + 16 * TILES)
                s_ = rows[z][:, :, 0:MUL]
                if n == 0:
                    qa = q_sb[z][:, 0:TILES * 3 * MUL].rearrange("p (t a i) -> p t a i", t=TILES, a=3)
                    nc.scalar.activation(qa[:, :, 2, :], s_, ACT.Copy).then_inc(s.rows_copied[z], 1)
                else:
                    q = q_sb[z][:].rearrange("p (t a i) -> p t a i", t=TILES, i=MUL)
                    nc.scalar.activation(q[:, :, 0, :], s_, ACT.Copy)
                    nc.scalar.activation(q[:, :, 2, :], s_, ACT.Copy).then_inc(s.rows_copied[z], 1)

            def complete_q(z, r):
                s = layers[1]
                q = q_sb[z][:].rearrange("p (t a i) -> p t a i", t=TILES, i=MUL)
                act.wait_ge(s.rows_read[z], r + 1)
                nc.scalar.activation(q[:, :, 1, :], q[:, :, 3, :], ACT.Copy).then_inc(s.q_completed[z], 1)

            def copy_plan(n, k, z, r, steps):
                act.wait_ge(layers[n].windows_split[z], r)
                steps.done(nc.scalar.activation(plan_sb[z][:], plan[:, bass.ds(k, 1), :].rearrange("p k c -> p (k c)"),
                                                ACT.Copy))

            def distances(n, z, r, half, steps):
                s = layers[n]
                if half == 0:
                    steps.need(steps.n)
                    act.wait_ge(s.onehot_ready[1 - z], r + z)
                for t in range(half * TILES // 2, (half + 1) * TILES // 2):
                    ins = nc.scalar.activation(gap[:, t, :], iota[:], ACT.Abs, bias=plan_sb[z][:, t:t + 1])
                steps.done(ins)

            def one_hots(n, z, steps):
                s = layers[n]
                for half in range(2):
                    steps.need(steps.n - 1 + half)
                    t0, t1 = half * TILES // 2, (half + 1) * TILES // 2
                    ins = nc.scalar.activation(onehot[z][:, t0:t1, :], gap[:, t0:t1, :], ACT.Relu, scale=-1.0, bias=1.0)
                ins.then_inc(s.onehot_ready[z], 1)

            def cut_first(n, z, r):
                s = layers[n]
                act.wait_ge(s.messages_ready[z], r + 1)
                nc.scalar.activation(parts[z][:, :, 0, :], msg[:], ACT.Copy).then_inc(s.part1_ready[z], 1)

            def cut_second(n, z, r):
                s = layers[n]
                act.wait_ge(s.rest_ready[z], r + 1)
                nc.scalar.activation(parts[z][:, :, 1, :], rest[:], ACT.Copy).then_inc(s.part2_ready[z], 1)

            def copy_sums(n, z, r):
                s = layers[n]
                a, b = (t * PATHS[n] * MUL for t in PE_TILES[n])
                act.wait_ge(s.products_summed[z], r + 1)
                nc.scalar.activation(sums[:, a:b], red[:, 0:b - a], ACT.Copy).then_inc(s.sums_copied[z], 1)

            def split_windows(n, z, r):
                s = layers[n]
                act.wait_ge(s.scattered[z], r + 1)
                for g in range(GROUPS):
                    for w in range(2):
                        ins = nc.scalar.activation(split[z][:, g, w * FEAT:(w + 1) * FEAT],
                                                   acc[z][:, g * FEAT:(g + 1) * FEAT], ACT.Identity,
                                                   scale=plan_sb[z][:, TILES + g * 2 + w:TILES + g * 2 + w + 1])
                ins.then_inc(s.windows_split[z], 1)

            def loop(n, count):
                s = layers[n]

                def body(i, z, r, last, steps):
                    k = i * RING + z
                    z1, r1 = next_chunk(z, r)
                    tail = last and z == RING - 1
                    if not tail:
                        copy_plan(n, k + 1, z1, r1, steps)
                        if n == 0:
                            copy_rows(n, i + z, z1, r1)
                        distances(n, z1, r1, 0, steps)
                    if not last:
                        load_geo(n, k + RING, z, r + 1)
                    cut_first(n, z, r)
                    if not tail:
                        distances(n, z1, r1, 1, steps)
                        if n == 0:
                            one_hots(n, z1, steps)
                    if n == 0:
                        cut_second(n, z, r)
                    if not last:
                        hide(n, z, r + 1, 0)
                        if n == 1:
                            hide(n, z, r + 1, 1)
                    if n == 1:
                        if not tail:
                            one_hots(n, z1, steps)
                        if not last:
                            copy_rows(n, i + 1, z, r + 1)
                    if n == 0:
                        split_windows(n, z, r)
                        if not last:
                            hide(n, z, r + 1, 1)
                    if n == 1 and not last:
                        complete_q(z, r + 1)
                    if not tail:
                        copy_sums(n, z1, r1)
                    if n == 1:
                        cut_second(n, z, r)
                        split_windows(n, z, r)

                with act.Fori(0, count) as j:
                    r0 = round_of(act, j, 0)
                    steps = Steps(act, s.act_steps, (r0 - 1) * (RING * 3))
                    act.wait_ge(s.counts_reset, j + 1)
                    for z in range(RING):
                        load_geo(n, z, z, r0)
                    for z in range(RING):
                        for half in range(2):
                            hide(n, z, r0, half)
                    act.wait_ge(windows_moved, (0 if n == 0 else count + 1) + j + 1)
                    copy_plan(n, 0, 0, r0, steps)
                    copy_rows(n, 0, 0, r0)
                    if n == 1:
                        complete_q(0, r0)
                    for half in range(2):
                        distances(n, 0, r0, half, steps)
                    one_hots(n, 0, steps)
                    if n == 1:
                        copy_rows(n, 0, 1, r0)
                    copy_sums(n, 0, r0)
                    if n == 1:
                        complete_q(1, r0)
                    with act.Fori(0, ROUNDS - 1) as i:
                        r = round_of(act, j, i)
                        steps = Steps(act, s.act_steps, (r - 1) * (RING * 3) + 3)
                        for z in range(RING):
                            body(i, z, r, False, steps)
                    r = round_of(act, j, ROUNDS - 1)
                    steps = Steps(act, s.act_steps, (r - 1) * (RING * 3) + 3)
                    for z in range(RING):
                        body(ROUNDS - 1, z, r, True, steps)

            def deviations(n):
                act.wait_ge(var_ready, n + 1)
                nc.scalar.activation(node_b[:], node_a[:], ACT.Sqrt, scale=1.0 / FEAT, bias=eps[:, 0:1]
                                     ).then_inc(std_ready, 1)

            spread_windows()
            act.wait_ge(loaded["weights"], 64)
            act.wait_ge(loaded["l1_weights"], 48)
            act.wait_ge(iota_ready, 1)
            act.wait_ge(consts_ready, 1)
            count = passes(act)
            loop(0, count)
            deviations(0)
            store_frames()
            for b in range(2):
                act.wait_ge(frames_stored[b], 16 * FRAME_PARTS // 2)
            loop(1, count)
            deviations(1)

        @block.tensor
        def _(pe):
            pe.wait_ge(loaded["self"], 32)
            for r in range(-(-SELF_CHUNKS // 4)):
                if r >= 4:
                    pe.wait_ge(self_added, r - 3)
                for c in range(4 * r, min(4 * r + 4, SELF_CHUNKS)):
                    col = (r % 4) * 512 + (c % 4) * P
                    ins = nc.tensor.matmul(wps[:, col:col + P], xs[:, c, :], si_sb[:], start=True, stop=True)
                ins.then_inc(self_ready, 1)

            def sum_hidden(n, z, r, half):
                s = layers[n]
                if half == 0:
                    pe.wait_ge(s.mlp_loaded[z], r * 16 + 16)
                    pe.wait_ge(s.hidden_ready[1 - z], (r + z) * 2)
                else:
                    pe.wait_ge(s.hidden_ready[z], r * 2 + 1)
                nc.tensor.matmul(hps[:], w1_sb[:, half, :], mlp_sb[z][:, 0:SET], start=True, stop=True
                                 ).then_inc(s.hidden_summed[z], 1)

            def weigh(n, z, r, halves, first=False):
                s = layers[n]
                H, T = HALVES[n], HALF_TILES[n]
                w2 = w2_sb[n][:].rearrange("p a c -> p (a c)")
                for q in halves:
                    if q == 0 or q == H // 2:
                        pe.wait_ge(s.hidden_ready[z], r * 2 + (1 if q == 0 else 2))
                    if q >= 2:
                        pe.wait_ge(s.weights_used[z], r * H + (q - 1))
                    elif first:
                        pe.wait_ge(s.weights_used[1 - z], r * H)
                    else:
                        pe.wait_ge(s.weights_used[1 - z], (r + z) * H + (q - 1))
                    for t in range(T):
                        col = (q % 2) * 1024 + t * (1024 // T)
                        e0 = (q * T + t) * P
                        ins = nc.tensor.matmul(wps[:, col:col + W_PATHS[n] * MM], hidden[:, z, e0:e0 + P], w2,
                                               start=True, stop=True)
                    ins.then_inc(s.weights_ready[z], 1)

            def sum_products(n, z, r):
                s = layers[n]
                a, b = (t * PATHS[n] * MM for t in PE_TILES[n])
                pr = prod[:, a:b].rearrange("p (o i) -> p i o", i=MUL)
                pe.wait_ge(s.weights_used[z], r * HALVES[n] + PE_HALVES[n])
                pe.wait_ge(s.sums_copied[1 - z], r + z)
                for i in range(MUL):
                    ins = nc.tensor.matmul(red[:, 0:(b - a) // MUL], ident[:], pr[:, i, :], start=(i == 0),
                                           stop=(i == MUL - 1))
                ins.then_inc(s.products_summed[z], 1)

            def scatter(n, z, r):
                s = layers[n]
                pe.wait_ge(s.onehot_ready[z], r + 1)
                pe.wait_ge(s.parts_ready[z], r + 1)
                pe.wait_ge(s.windows_split[z], r)
                for t in range(TILES):
                    g, tg = divmod(t, GROUP_TILES)
                    for part in range(3):
                        ins = nc.tensor.matmul(acc[z][:, g * FEAT:(g + 1) * FEAT], onehot[z][:, t, :],
                                               parts[z][:, t, part, :], start=(tg == 0 and part == 0),
                                               stop=(tg == GROUP_TILES - 1 and part == 2))
                ins.then_inc(s.scattered[z], 1)

            def loop(n, count):
                H = HALVES[n]

                def body(z, r, last):
                    z1, r1 = next_chunk(z, r)
                    if last and z == RING - 1:
                        scatter(n, z, r)
                        return
                    if n == 0:
                        weigh(n, z1, r1, range(2, H))
                        if not last:
                            sum_hidden(n, z, r + 1, 0)
                        scatter(n, z, r)
                        if not last:
                            sum_hidden(n, z, r + 1, 1)
                        sum_products(n, z1, r1)
                        if not last:
                            weigh(n, z, r + 1, (0, 1))
                    else:
                        weigh(n, z1, r1, range(2, H - 2))
                        sum_products(n, z1, r1)
                        weigh(n, z1, r1, range(H - 2, H))
                        if not last:
                            weigh(n, z, r + 1, (0, 1))
                        scatter(n, z, r)

                with pe.Fori(0, count) as j:
                    r0 = round_of(pe, j, 0)
                    if n == 0:
                        for half in range(2):
                            sum_hidden(n, 0, r0, half)
                    weigh(n, 0, r0, (0, 1), True)
                    if n == 0:
                        for half in range(2):
                            sum_hidden(n, 1, r0, half)
                    weigh(n, 0, r0, range(2, H))
                    sum_products(n, 0, r0)
                    weigh(n, 1, r0, (0, 1))
                    with pe.Fori(0, ROUNDS - 1) as i:
                        r = round_of(pe, j, i)
                        for z in range(RING):
                            body(z, r, False)
                    r = round_of(pe, j, ROUNDS - 1)
                    for z in range(RING):
                        body(z, r, True)

            pe.wait_ge(loaded["weights"], 64)
            pe.wait_ge(consts_ready, 1)
            pe.wait_ge(w2_scaled, 1)
            pe.wait_ge(hidden_filled, 2)
            count = passes(pe)
            loop(0, count)
            loop(1, count)

        @block.vector
        def _(dve):
            st = Steps(dve, setup_steps)

            def chain(instruction):
                st.need(st.done(instruction))

            ROWS = N_GROUPS // 4
            st.done(nc.vector.memset(span_max[:], -1.0))
            st.done(nc.vector.memset(lowest[:], 0.0))
            dve.wait_ge(loaded["dst_rows"], 16)
            node = work[0:ROWS, 0:4 * GROUP]
            pad = work[0:ROWS, 4 * GROUP:8 * GROUP]
            chain(nc.vector.tensor_copy(node, dst_i[0:ROWS, :]))
            st.done(nc.vector.tensor_scalar(pad, node, 0.0, FAR, ALU.is_lt, ALU.mult))
            chain(nc.vector.tensor_reduce(highest[0:ROWS, :], node.rearrange("r (g e) -> r g e", g=4), AX_X, ALU.max))
            chain(nc.vector.tensor_tensor(node, node, pad, ALU.add))
            chain(nc.vector.tensor_reduce(lowest[0:ROWS, :], node.rearrange("r (g e) -> r g e", g=4), AX_X, ALU.min))
            chain(nc.vector.tensor_tensor(span[0:ROWS, :], highest[0:ROWS, :], lowest[0:ROWS, :], ALU.subtract))
            nc.vector.tensor_reduce(span_max[0:ROWS, 0:1], span[0:ROWS, :], AX_X, ALU.max).then_inc(spans_reduced, 1)
            chain(nc.vector.tensor_scalar(lowest[:], lowest[:], float(N_NODES - 1), None, ALU.min))

            dve.wait_ge(spans_known, 1)
            chain(nc.vector.tensor_scalar(fits[:], span_max[:, 1:2], float(P) - 0.5, None, ALU.is_lt))
            chain(nc.vector.tensor_scalar(passes_f[:], fits[:], float(1 - PASSES_ALL), float(PASSES_ALL),
                                          ALU.mult, ALU.add))
            st.done(nc.vector.tensor_copy(passes_i[:], passes_f[:]))
            chain(nc.vector.tensor_scalar(lowest[:], lowest[:], fits[:, 0:1], None, ALU.mult))
            chain(nc.vector.tensor_copy(start_i[:], lowest[:]))
            st.done(nc.vector.tensor_scalar(off_i[:], start_i[:], 7, 5, ALU.arith_shift_right, ALU.logical_shift_left))
            chain(nc.vector.tensor_single_scalar(rem_i[:], start_i[:], P - 1, ALU.bitwise_and))
            chain(nc.vector.tensor_copy(rem_f[:], rem_i[:]))
            dve.nop().then_inc(windows_known, 1)

            dve.wait_ge(loaded["weights"], 64)
            chain(nc.vector.tensor_scalar(w2_sb[0][:], w2_sb[0][:], ALPHA, None, ALU.mult))
            st.done(nc.vector.tensor_scalar(w2_sb[0][:, 1, :], w2_sb[0][:, 1, :], C110, None, ALU.mult))
            dve.wait_ge(loaded["l1_weights"], 48)
            w2 = w2_sb[1]
            for path, factor in ((3, K_11_2), (0, K_00), (1, K_01), (2, K_10), (6, K_11_1)):
                st.done(nc.vector.tensor_scalar(w2[:, path, :], w2[:, path, :], factor, None, ALU.mult))
            st.need(st.n)
            chain(nc.vector.tensor_scalar(w2_tmp[:], w2[:, 3, :], -1.0 / 3.0, None, ALU.mult))
            chain(nc.vector.scalar_tensor_tensor(out=w2[:, 4, :], in0=w2[:, 4, :], scalar=K_11_0, in1=w2_tmp[:],
                                                 op0=ALU.mult, op1=ALU.add))
            st.done(nc.vector.tensor_tensor(w2[:, 3, :], w2[:, 3, :], w2[:, 4, :], ALU.add))
            chain(nc.vector.tensor_tensor(w2[:, 5, :], w2[:, 4, :], w2[:, 6, :], ALU.add))
            chain(nc.vector.tensor_tensor(w2[:, 4, :], w2[:, 4, :], w2[:, 6, :], ALU.subtract))
            dve.nop().then_inc(w2_scaled, 1)

            dve.wait_ge(loaded["nodes"], 16)
            st.done(nc.vector.memset(table[:, BLOCKS, :], 0.0))
            for r in range(-(-SELF_CHUNKS // 4)):
                dve.wait_ge(self_ready, r + 1)
                b0, b1 = 16 * r, min(16 * r + 16, BLOCKS)
                nc.vector.scalar_tensor_tensor(
                    out=table[:, b0:b1, :],
                    in0=wps[:, (r % 4) * 512:(r % 4) * 512 + (b1 - b0) * FEAT].rearrange("p (b f) -> p b f", f=FEAT),
                    scalar=SI_SCALE, in1=table[:, b0:b1, :], op0=ALU.mult, op1=ALU.add).then_inc(self_added, 1)
            dve.wait_ge(self_added, -(-SELF_CHUNKS // 4))
            st.done(nc.vector.memset(eps[:], LN_EPS))
            st.need(st.n)
            dve.nop().then_inc(consts_ready, 1)

            dve.wait_ge(loaded["dst"], 16)
            target = work[:, 0:CHUNKS * TILES]
            rest_ = work[:, CHUNKS * TILES:2 * CHUNKS * TILES]
            chain(nc.vector.tensor_copy(target, dst_t[:]))
            chain(nc.vector.tensor_single_scalar(dst_t[:], dst_t[:], P - 1, ALU.bitwise_and))
            negkey0 = plan0[:, :, 0:TILES]

            def by_chunk(ap):
                return ap.rearrange("p (k t) -> p k t", t=TILES)

            st.done(nc.vector.tensor_scalar(negkey0, by_chunk(target), 0.0, FAR, ALU.is_lt, ALU.mult))
            chain(nc.vector.tensor_copy(rest_, dst_t[:]))
            chain(nc.vector.tensor_tensor(rest_, target, rest_, ALU.subtract))
            st.done(nc.vector.tensor_tensor(negkey0, negkey0, by_chunk(target), ALU.subtract))
            chain(nc.vector.tensor_scalar(rest_, rest_, fits[:, 0:1], None, ALU.mult))
            chain(nc.vector.tensor_tensor(negkey0, negkey0, by_chunk(rest_), ALU.add))

            st.done(nc.vector.memset(offs0[:, 0:GROUPS], 0))
            dve.wait_ge(iota_ready, 1)
            dve.wait_ge(loaded["rem"], 16)
            masks = plan0[:, :, TILES:PLAN].rearrange("p k (g w) -> p k g w", w=2)
            rem_g = rem_sb[:].rearrange("p (k g) -> p k g", g=GROUPS)
            st.done(nc.vector.tensor_scalar(masks[:, :, :, 0], rem_g, iota_p[:, 0:1], None, ALU.is_le))
            chain(nc.vector.tensor_scalar(masks[:, :, :, 1], rem_g, iota_p[:, 0:1], None, ALU.is_gt))

            dve.wait_ge(loaded["offs"], 16)

            def make_frames():
                lengths = work[:, 0:CHUNKS * TILES]
                inverse = work[:, CHUNKS * TILES:2 * CHUNKS * TILES]
                sq = prod[:, 0:CHUNKS * TILES * 3].rearrange("p (t c) -> p t c", c=3)
                dve.wait_ge(loaded["rel"], 16)
                chain(nc.vector.tensor_tensor(sq, rel_sb[:], rel_sb[:], ALU.mult))
                nc.vector.tensor_reduce(lengths, sq, AX_X, ALU.add).then_inc(lengths_squared, 1)
                dve.wait_ge(lengths_ready, 1)
                chain(nc.vector.reciprocal(inverse, lengths))
                sign, tmp = (t_a[:, c * PART_TILES:(c + 1) * PART_TILES] for c in range(2))
                h, tmp2 = (t_b[:, c * PART_TILES:(c + 1) * PART_TILES] for c in range(2))
                for part in range(FRAME_PARTS):
                    frame = prod[:, part % 2 * PART_TILES * GEO[1]:(part % 2 + 1) * PART_TILES * GEO[1]].rearrange(
                        "p (t c) -> p t c", c=GEO[1])
                    u0, u1, u2, a0, a1, a2, b0_, b1_, b2_ = (frame[:, :, c] for c in range(GEO[1]))
                    vec = rel_sb[:, part * PART_TILES:(part + 1) * PART_TILES, :]
                    inv = inverse[:, part * PART_TILES:(part + 1) * PART_TILES]
                    if part >= 2:
                        dve.wait_ge(frames_stored[part % 2], 16 * (part // 2))
                    st.done(nc.vector.tensor_tensor(frame[:, :, 0:2], vec[:, :, 1:3],
                                                    inv.unsqueeze(2).broadcast_to([P, PART_TILES, 2]), ALU.mult))
                    chain(nc.vector.tensor_tensor(u2, vec[:, :, 0], inv, ALU.mult))
                    chain(nc.vector.tensor_scalar(sign, u2, 0.0, 2.0, ALU.is_ge, ALU.mult))
                    chain(nc.vector.tensor_scalar(sign, sign, -1.0, None, ALU.add))
                    chain(nc.vector.tensor_tensor(h, sign, u2, ALU.add))
                    st.done(nc.vector.scalar_tensor_tensor(out=a2, in0=u0, scalar=-1.0, in1=sign, op0=ALU.mult,
                                                           op1=ALU.mult))
                    chain(nc.vector.reciprocal(h, h))
                    st.done(nc.vector.tensor_scalar(b2_, u1, -1.0, None, ALU.mult))
                    st.done(nc.vector.tensor_tensor(tmp, u0, h, ALU.mult))
                    chain(nc.vector.tensor_tensor(tmp2, u1, h, ALU.mult))
                    st.done(nc.vector.tensor_tensor(tmp, a2, tmp, ALU.mult))
                    chain(nc.vector.scalar_tensor_tensor(out=b0_, in0=u0, scalar=-1.0, in1=tmp2, op0=ALU.mult,
                                                         op1=ALU.mult))
                    st.done(nc.vector.tensor_tensor(tmp2, u1, tmp2, ALU.mult))
                    st.done(nc.vector.tensor_tensor(a1, sign, b0_, ALU.mult))
                    chain(nc.vector.tensor_scalar(a0, tmp, 1.0, None, ALU.add))
                    chain(nc.vector.tensor_tensor(b1_, sign, tmp2, ALU.subtract))
                    dve.nop().then_inc(frames_ready, 1)

                for b in range(2):
                    dve.wait_ge(frames_stored[b], 16 * FRAME_PARTS // 2)


            flat = table[:].rearrange("p b f -> p (b f)")

            def vec_im(ap):
                return ap.rearrange("p t (i m) -> p t i m", m=3)

            def vec_mi(ap):
                return ap.rearrange("p t (i m) -> p t m i", m=3)

            def q_a(z):
                return q_sb[z][:, 0:TILES * 3 * MUL].rearrange("p (t a i) -> p t a i", t=TILES, a=3)

            def q_b(z):
                return q_sb[z][:, TILES * 3 * MUL:TILES * 6 * MUL].rearrange("p (t m i) -> p t m i", t=TILES, m=3)

            def q_all(z):
                return q_sb[z][:].rearrange("p (t a i) -> p t a i", t=TILES, i=MUL)

            def harmonics(z):
                return geo_sb[z][:, 0:TILES * GEO[0]].rearrange("p (t c) -> p t c", c=GEO[0])

            def frames(z):
                return geo_sb[z][:].rearrange("p (t f m) -> p t f m", t=TILES, m=3)

            def sums_of(n):
                return sums[:, 0:TILES * PATHS[n] * MUL].rearrange("p (t a o) -> p t a o", t=TILES, o=MUL)

            def multiply(n, z, r, q):
                s = layers[n]
                T = HALF_TILES[n]
                t0 = q * T
                C = PATHS[n] * MM
                w = wps[:, (q % 2) * 1024:(q % 2) * 1024 + 1024].rearrange("p (t c) -> p t c", t=T)
                pr = prod[:, t0 * C:(t0 + T) * C].rearrange("p (t c) -> p t c", t=T)
                dve.wait_ge(s.weights_ready[z], r * HALVES[n] + q + 1)
                if n == 0:
                    nc.vector.tensor_tensor(
                        pr[:, :, 3 * MM:6 * MM].rearrange("p t (m o i) -> p t m o i", m=3, o=MUL),
                        w[:, :, 3 * MM:4 * MM].rearrange("p t (o i) -> p t o i", o=MUL).unsqueeze(2)
                        .broadcast_to([P, T, 3, MUL, MUL]),
                        q_b(z)[:, t0:t0 + T].unsqueeze(3).broadcast_to([P, T, 3, MUL, MUL]), ALU.mult)
                    if q == 0:
                        dve.wait_ge(s.rows_copied[z], r + 1)
                    ins = nc.vector.tensor_tensor(
                        pr[:, :, 0:3 * MM].rearrange("p t (a o i) -> p t a o i", a=3, o=MUL),
                        w[:, :, 0:3 * MM].rearrange("p t (a o i) -> p t a o i", a=3, o=MUL),
                        q_a(z)[:, t0:t0 + T].unsqueeze(3).broadcast_to([P, T, 3, MUL, MUL]), ALU.mult)
                else:
                    if q == 0:
                        dve.wait_ge(s.q_completed[z], r + 1)
                    ins = nc.vector.tensor_tensor(
                        pr.rearrange("p t (a o i) -> p t a o i", a=7, o=MUL),
                        w[:, :, 0:C].rearrange("p t (a o i) -> p t a o i", a=7, o=MUL),
                        q_all(z)[:, t0:t0 + T].unsqueeze(3).broadcast_to([P, T, 7, MUL, MUL]), ALU.mult)
                ins.then_inc(s.weights_used[z], 1)

            def sum_tiles(n, z, r, which, st):
                s = layers[n]
                t0, t1 = DVE_SUMS[n][which]
                C = PATHS[n] * MM
                dve.wait_ge(s.weights_used[z], r * HALVES[n] + -(-t1 // HALF_TILES[n]))
                st.done(nc.vector.tensor_reduce(
                    sums[:, t0 * PATHS[n] * MUL:t1 * PATHS[n] * MUL],
                    prod[:, t0 * C:t1 * C].rearrange("p (o i) -> p o i", i=MUL), AX_X, ALU.add))

            def first_rest(z, r):
                s = layers[0]
                dve.wait_ge(s.part1_ready[z], r + 1)
                nc.vector.tensor_tensor(rest[:], msg[:], parts[z][:, :, 0, :], ALU.subtract).then_inc(s.rest_ready[z], 1)

            def last_part(z, r):
                s = layers[0]
                dve.wait_ge(s.part2_ready[z], r + 1)
                nc.vector.tensor_tensor(parts[z][:, :, 2, :], rest[:], parts[z][:, :, 1, :], ALU.subtract
                                        ).then_inc(s.parts_ready[z], 1)

            def project(n, i, z, r, st):
                s = layers[n]
                dve.wait_ge(s.geo_loaded[z], r * 16 + 16)
                dve.wait_ge(s.rows_gathered[z], i * (16 * TILES) + 16 * TILES)
                v_ = rows[z][:, :, MUL:FEAT]
                if n == 0:
                    ins = nc.vector.tensor_tensor(
                        vec_im(t_a[:, 0:TILES * 3 * MUL].rearrange("p (t c) -> p t c", t=TILES)), vec_im(v_),
                        harmonics(z)[:, :, 1:4].unsqueeze(2).broadcast_to([P, TILES, MUL, 3]), ALU.mult)
                else:
                    ins = nc.vector.tensor_tensor(
                        t_a[:].rearrange("p (t f i m) -> p t f i m", t=TILES, f=3, m=3),
                        vec_im(v_).unsqueeze(2).broadcast_to([P, TILES, 3, MUL, 3]),
                        frames(z).unsqueeze(3).broadcast_to([P, TILES, 3, MUL, 3]), ALU.mult)
                return st.done(ins)

            def project_sum(n, z):
                s = layers[n]
                if n == 0:
                    ins = nc.vector.tensor_reduce(
                        q_a(z)[:, :, 1, :], t_a[:, 0:TILES * 3 * MUL].rearrange("p (t i m) -> p t i m", t=TILES, m=3),
                        AX_X, ALU.add)
                else:
                    ins = nc.vector.tensor_reduce(
                        q_sb[z][:].rearrange("p (t c) -> p t c", t=TILES)[:, :, 3 * MUL:6 * MUL],
                        t_a[:].rearrange("p (t c m) -> p t c m", t=TILES, m=3), AX_X, ALU.add)
                ins.then_inc(s.rows_read[z], 1)

            def scale_rows(z, st):
                sh0 = harmonics(z)[:, :, 0:1]
                st.done(nc.vector.tensor_tensor(q_a(z)[:, :, 0, :], rows[z][:, :, 0:MUL],
                                                sh0.broadcast_to([P, TILES, MUL]), ALU.mult))
                return st.done(nc.vector.tensor_tensor(q_b(z), vec_mi(rows[z][:, :, MUL:FEAT]),
                                                       sh0.unsqueeze(3).broadcast_to([P, TILES, 3, MUL]), ALU.mult))

            def differ(z, r, st):
                dve.wait_ge(layers[1].rows_read[z], r + 1)
                q = q_all(z)
                return st.done(nc.vector.tensor_tensor(q[:, :, 6, :], q[:, :, 4, :], q[:, :, 5, :], ALU.subtract))

            def add_window(g, cols, z, st):
                if g:
                    st.need(add_window.last)
                window = flat[:, bass.ds(cols[g], 2 * FEAT)]
                add_window.last = st.done(nc.vector.tensor_tensor(window, window, split[z][:, g, :], ALU.add))

            def load_columns(k):
                _, cols = nc.values_load_multi_w_load_instructions(
                    offs[0:1, bass.ds(k * GROUPS, GROUPS)], engines=(mybir.EngineType.DVE,), min_val=0,
                    max_val=(BLOCKS - 1) * FEAT)
                return cols

            def body0(i, z, r, st, tail):
                s = layers[0]
                k = i * RING + z
                z1, r1 = next_chunk(z, r)
                sm = sums_of(0)
                cols = load_columns(k)
                if not tail:
                    projected = project(0, i + z, z1, r1, st)
                st.need(0)
                dve.wait_ge(s.windows_split[z1], r + z)
                add_window(0, cols, z1, st)
                add_window(1, cols, z1, st)
                if not tail:
                    scaled = scale_rows(z1, st)
                add_window(2, cols, z1, st)
                if not tail:
                    st.need(projected)
                    project_sum(0, z1)
                along = t_b[:, 0:TILES * 3 * MUL].rearrange("p (t o m) -> p t o m", t=TILES, m=3)
                dve.wait_ge(s.sums_copied[z], r + 1)
                nc.vector.tensor_tensor(
                    along, sm[:, :, 2, :].unsqueeze(3).broadcast_to([P, TILES, MUL, 3]),
                    harmonics(z)[:, :, 1:4].unsqueeze(2).broadcast_to([P, TILES, MUL, 3]), ALU.mult
                ).then_inc(s.geo_used[z], 1)
                nc.vector.tensor_tensor(msg[:, :, 0:MUL], sm[:, :, 0, :], sm[:, :, 1, :], ALU.add)
                add_window(3, cols, z1, st)
                dve.wait_ge(s.geo_used[z], r + 1)
                nc.vector.tensor_tensor(
                    vec_im(msg[:, :, MUL:FEAT]), along, sm[:, :, 3:6, :].rearrange("p t m o -> p t o m"), ALU.add
                ).then_inc(s.messages_ready[z], 1)
                if not tail:
                    st.need(scaled)
                    dve.wait_ge(s.rows_read[z1], r1 + 1)
                    multiply(0, z1, r1, 0)
                    multiply(0, z1, r1, 1)
                first_rest(z, r)
                if not tail:
                    multiply(0, z1, r1, 2)
                last_part(z, r)
                if not tail:
                    multiply(0, z1, r1, 3)
                    for which in range(len(DVE_SUMS[0])):
                        sum_tiles(0, z1, r1, which, st)

            def prologue0(r, st):
                projected = project(0, 0, 0, r, st)
                scaled = scale_rows(0, st)
                st.need(projected)
                project_sum(0, 0)
                st.need(scaled)
                dve.wait_ge(layers[0].rows_read[0], r + 1)
                for q in range(HALVES[0]):
                    multiply(0, 0, r, q)
                for which in range(len(DVE_SUMS[0])):
                    sum_tiles(0, 0, r, which, st)

            def body1(i, z, r, st, last, tail):
                s = layers[1]
                k = i * RING + z
                z1, r1 = next_chunk(z, r)
                sm = sums_of(1)
                if not tail:
                    st.need(-1)
                    multiply(1, z1, r1, 0)
                st.need(0)
                dve.wait_ge(s.sums_copied[z], r + 1)
                dve.wait_ge(s.rest_ready[z1], r + z)
                pair = sm[:, :, 0:4, :].rearrange("p t (b a) o -> p t b a o", a=2)
                st.done(nc.vector.tensor_tensor(
                    msg[:, :, 0:2 * MUL].rearrange("p t (b o) -> p t b o", b=2), pair[:, :, :, 0, :],
                    pair[:, :, :, 1, :], ALU.add))
                if not tail:
                    multiply(1, z1, r1, 1)
                framed = st.done(nc.vector.tensor_tensor(
                    msg[:, :, 2 * MUL:FEAT].rearrange("p t (b o) -> p t b o", b=2), sm[:, :, 4:6, :],
                    sm[:, :, 6:7, :].broadcast_to([P, TILES, 2, MUL]), ALU.add))
                if not tail:
                    multiply(1, z1, r1, 2)
                st.need(framed)
                turned = t_b[:].rearrange("p (t f c) -> p t f c", t=TILES, f=3)
                nc.vector.tensor_tensor(
                    turned.rearrange("p t f (o m) -> p t f o m", m=3),
                    msg[:, :, MUL:FEAT].rearrange("p t (f o) -> p t f o", f=3).unsqueeze(4)
                    .broadcast_to([P, TILES, 3, MUL, 3]),
                    frames(z).unsqueeze(3).broadcast_to([P, TILES, 3, MUL, 3]), ALU.mult).then_inc(s.geo_used[z], 1)
                if not tail:
                    multiply(1, z1, r1, 3)
                    multiply(1, z1, r1, 4)
                dve.wait_ge(s.geo_used[z], r + 1)
                nc.vector.tensor_reduce(msg[:, :, MUL:FEAT], turned.rearrange("p t f c -> p t c f"), AX_X, ALU.add
                                        ).then_inc(s.messages_ready[z], 1)
                if not tail:
                    multiply(1, z1, r1, 5)
                if not last:
                    projected = project(1, i + 1, z, r + 1, st)
                cols = load_columns(k)
                dve.wait_ge(s.windows_split[z1], r + z)
                add_window(0, cols, z1, st)
                if not last:
                    st.need(projected)
                    project_sum(1, z)
                add_window(1, cols, z1, st)
                if not tail:
                    sum_tiles(1, z1, r1, 0, st)
                add_window(2, cols, z1, st)
                if not tail:
                    multiply(1, z1, r1, 6)
                add_window(3, cols, z1, st)
                if not tail:
                    multiply(1, z1, r1, 7)
                if not last:
                    differ(z, r + 1, st)
                if not tail:
                    sum_tiles(1, z1, r1, 1, st)

            def prologue1(r, st):
                for z in range(RING):
                    st.need(project(1, 0, z, r, st))
                    project_sum(1, z)
                    st.need(differ(z, r, st))
                for q in range(HALVES[1]):
                    multiply(1, 0, r, q)
                for which in range(len(DVE_SUMS[1])):
                    sum_tiles(1, 0, r, which, st)

            def body(n, i, z, r, st, last, tail):
                if n == 0:
                    body0(i, z, r, st, tail)
                else:
                    body1(i, z, r, st, last, tail)

            def loop(n, count):
                s = layers[n]
                with dve.Fori(0, count) as j:
                    r0 = round_of(dve, j, 0)
                    st = Steps(dve, s.dve_prologue, j * PROLOGUE_STEPS[n])
                    dve.wait_ge(s.counts_reset, j + 1)
                    st.need(st.done(nc.vector.memset(split[1][:], 0.0)))
                    (prologue0, prologue1)[n](r0, st)
                    assert st.n == PROLOGUE_STEPS[n], ("prologue", n, st.n)
                    st.need(st.n)
                    dve.sem_inc(dve_turns, 1)
                    bodies = CHUNKS - 1
                    with dve.Fori(0, ROUNDS - 1) as i:
                        r = round_of(dve, j, i)
                        for z in range(RING):
                            st = Steps(dve, s.dve_body, j * (bodies * BODY_STEPS[n])
                                       + i * (RING * BODY_STEPS[n]) + (z + 1) * BODY_STEPS[n])
                            body(n, i, z, r, st, False, False)
                            assert st.n == BODY_STEPS[n], ("body", n, st.n)
                    r = round_of(dve, j, ROUNDS - 1)
                    st = Steps(dve, s.dve_body, j * (bodies * BODY_STEPS[n]) + bodies * BODY_STEPS[n])
                    body(n, ROUNDS - 1, 0, r, st, True, False)
                    for _ in range(st.n, BODY_STEPS[n]):
                        st.done(dve.nop())
                    st.need(st.n)
                    dve.sem_inc(dve_turns, 1)
                    st = Steps(dve, s.dve_tail, j * TAIL_STEPS[n])
                    body(n, ROUNDS - 1, 1, r, st, True, True)
                    cols = load_columns(CHUNKS)
                    dve.wait_ge(s.windows_split[1], r + 1)
                    st.need(st.n)
                    for g in range(GROUPS):
                        add_window(g, cols, 1, st)
                    st.need(st.n)
                    dve.wait_ge(s.onehot_ready[1], r + 1)
                    st.done(nc.vector.tensor_scalar(offs[:], offs[:], FEAT, None, ALU.add))
                    st.done(nc.vector.tensor_scalar(plan[:, :, 0:TILES], plan[:, :, 0:TILES], float(P), None, ALU.add))
                    assert st.n == TAIL_STEPS[n], ("tail", n, st.n)
                    st.need(st.n)
                    dve.nop().then_inc(windows_moved, 1)

            def first_windows():
                st.done(nc.vector.tensor_copy(offs[:], offs0[:]))
                chain(nc.vector.tensor_copy(plan[:], plan0[:]))
                dve.nop().then_inc(windows_moved, 1)

            def normalize(n):
                nodes = table[:, 0:BLOCKS, :]
                sq_ = work[:, 0:BLOCKS * FEAT].rearrange("p (b f) -> p b f", f=FEAT)
                chain(nc.vector.tensor_reduce(node_a[:], nodes, AX_X, ALU.add))
                chain(nc.vector.tensor_scalar(node_c[:], node_a[:], 1.0 / FEAT, None, ALU.mult))
                chain(nc.vector.tensor_tensor(nodes, nodes, node_c[:].unsqueeze(2).broadcast_to([P, BLOCKS, FEAT]),
                                              ALU.subtract))
                chain(nc.vector.tensor_tensor(sq_, nodes, nodes, ALU.mult))
                nc.vector.tensor_reduce(node_a[:], sq_, AX_X, ALU.add).then_inc(var_ready, 1)
                dve.wait_ge(std_ready, n + 1)
                chain(nc.vector.reciprocal(node_c[:], node_b[:]))
                nc.vector.tensor_tensor(nodes, nodes, node_c[:].unsqueeze(2).broadcast_to([P, BLOCKS, FEAT]),
                                        ALU.mult).then_inc(nodes_ready, 1)

            for n, s in enumerate(layers):
                dve.sem_inc(s.dve_body, BODY_STEPS[n])
            first_windows()
            count = passes(dve)
            loop(0, count)
            normalize(0)
            make_frames()
            first_windows()
            dve.wait_ge(x1_stored, 16)
            loop(1, count)
            normalize(1)


_OUT = ((N_NODES, FEAT), "float32")


def kernel(x, src, dst, edge_attr_3, edge_attr_32, edge_attr_4, edge_weight, L0_gnn_W1, L0_gnn_b1, L0_gnn_W2,
           L0_gnn_b2, L0_gnn_si_w0, L0_gnn_si_w1, L1_gnn_w1, L1_gnn_b1, L1_gnn_w2, L1_gnn_b2):
    import concourse.bacc as bacc
    from concourse.bass_utils import run_bass_kernel_spmd

    def padded(a, n, value):
        a = np.asarray(a)
        return np.concatenate([a, np.full((n - a.shape[0], *a.shape[1:]), value, a.dtype)])

    def by_partition(a):
        return np.swapaxes(a.reshape(CHUNKS, TILES, P, *a.shape[1:]), 1, 2)

    def all_by_partition(a):
        return np.swapaxes(by_partition(a), 0, 1).reshape(P, CHUNKS * TILES, *a.shape[1:])

    x = np.asarray(x)
    x_pad = padded(x, SELF_CHUNKS * 4 * P, 0)
    dst_p = padded(dst, EDGES, -1)
    feat = padded(edge_attr_32, EDGES, 0).reshape(CHUNKS, SETS, SET, FEAT)
    W1 = np.zeros((SETS, FEAT, 2, 2, HID), np.float32)
    for s in range(SETS):
        W1[s, :, s // 2, s % 2, :] = np.asarray(L0_gnn_W1)
    b1_0 = np.asarray(L0_gnn_b1).reshape(HID, 1)
    S = np.zeros((4, FEAT, 4, FEAT), np.float32)
    for b in range(4):
        S[b, :MUL, b, :MUL] = np.asarray(L0_gnn_si_w0)
        for m in range(3):
            S[b, MUL + m::3, b, MUL + m::3] = np.asarray(L0_gnn_si_w1)

    def with_bias(w, b, paths):
        cols = np.concatenate([c.ravel() for c in paths])
        out = np.zeros((P, len(cols)), np.float32)
        out[:HID] = np.asarray(w)[:, cols]
        out[HID] = np.asarray(b)[cols]
        return out.reshape(P, len(paths), MM)

    i, o = np.arange(MUL)[None, :], np.arange(MUL)[:, None]
    w000, w011, w101, w110 = (p * MM + i * MUL + o for p in range(4))
    uv = o * MUL + i
    R00, R01, R10 = uv, MM + uv, 2 * MM + uv
    R0, R1, R2 = (3 * MM + uv * 3 + l for l in range(3))

    arrays = {
        "x": x,
        "x_nodes": np.swapaxes(x_pad[:BLOCKS * P].reshape(BLOCKS, P, FEAT), 0, 1),
        "x_self": x_pad.reshape(SELF_CHUNKS, 4, P, FEAT).transpose(1, 3, 0, 2).reshape(P, SELF_CHUNKS, P),
        "src": by_partition(padded(src, EDGES, 0)),
        "dst": all_by_partition(dst_p),
        "dst_rows": dst_p.reshape(N_GROUPS // 4, 4 * GROUP),
        "sh": by_partition(padded(edge_attr_4, EDGES, 0)).reshape(CHUNKS, P, TILES * GEO[0]),
        "feat": np.swapaxes(feat, 2, 3).reshape(CHUNKS, P, SET),
        "rel": all_by_partition(padded(edge_attr_3, EDGES, 1)),
        "dist": padded(edge_weight, EDGES, 0).reshape(CHUNKS, CHUNK),
        "identity": np.eye(P, dtype=np.float32),
        "w1_0": W1.reshape(P, 2, 2 * HID),
        "b1_0": np.concatenate([b1_0, b1_0]),
        "w2_0": with_bias(L0_gnn_W2, L0_gnn_b2, (w000, w110, w011, w101)),
        "si": S.reshape(P, P),
        "w1_1": np.asarray(L1_gnn_w1).reshape(HID, 1),
        "b1_1": np.asarray(L1_gnn_b1).reshape(HID, 1),
        "w2_1": with_bias(L1_gnn_w2, L1_gnn_b2, (R00, R01, R10, R2, R0, R0, R1)),
    }
    nc = bacc.Bacc("TRN2", target_bir_lowering=False, num_devices=1)
    args, ins = {}, {}
    for name, a in arrays.items():
        ins[f"in_{name}"] = np.ascontiguousarray(a)
        args[name] = nc.dram_tensor(f"in_{name}", a.shape, mybir.dt.from_np(a.dtype), kind="ExternalInput").ap()
    out = nc.dram_tensor("out_0", _OUT[0], F32, kind="ExternalOutput").ap()
    build(nc, out=out, **args)
    r = run_bass_kernel_spmd(nc, [ins], core_ids=[0])
    return r.results[0]["out_0"]
```
